# Optimizing a Trainium2 kernel written in Bass

```python
import numpy as np
import jax
import jax.numpy as jnp

def _softmax(x, axis=-1):
    return jax.nn.softmax(x, axis=axis)

def _gelu(x):
    return jax.nn.gelu(x, approximate=True)

def _silu(x):
    return jax.nn.silu(x)

def _sigmoid(x):
    return jax.nn.sigmoid(x)

def _layernorm(x, axis=-1, eps=1e-05):
    m = jnp.mean(x, axis=axis, keepdims=True)
    v = jnp.var(x, axis=axis, keepdims=True)
    return (x - m) / jnp.sqrt(v + eps)

def _scatter_add(tgt, idx, src, axis=0):
    return tgt.at[idx].add(src)

def _segment_sum(src, seg, n):
    return jax.ops.segment_sum(src, seg, n)
kernel_name = 'mk_sandwich_d2_jaxref_r8_0da542'

def setup_inputs(seed: int=0):
    np.random.seed(seed)
    _w = jnp.asarray

    def _L0_attn_setup():
        import jax, jax.numpy as jnp
        import numpy as np
        import math
        N_HEAD = 16
        N_KV_HEAD = 4
        HEAD_DIM = 64
        ROPE_THETA = 10000.0

        def _rope_cache(T, D, dtype):
            inv_freq = 1.0 / ROPE_THETA ** (jnp.arange(0, D, 2, dtype=dtype) / D)
            t = jnp.arange(T, dtype=dtype)
            freqs = jnp.einsum('i,j->ij', t, inv_freq)
            return (jnp.cos(freqs)[None, None], jnp.sin(freqs)[None, None])

        def _apply_rope(x, cos, sin):
            x1 = x[..., ::2]
            x2 = x[..., 1::2]
            return jnp.concatenate([x1 * cos - x2 * sin, x1 * sin + x2 * cos], axis=-1)
        key = jax.random.key(seed)
        k0, k1, k2, k3, k4 = jax.random.split(key, 5)
        B, T, C = (4, 256, 128)
        scale = 0.02
        return {'x': jax.random.normal(k0, (B, T, C), dtype=jnp.float32), 'Wq': jax.random.normal(k1, (C, N_HEAD * HEAD_DIM), dtype=jnp.float32) * scale, 'Wk': jax.random.normal(k2, (C, N_KV_HEAD * HEAD_DIM), dtype=jnp.float32) * scale, 'Wv': jax.random.normal(k3, (C, N_KV_HEAD * HEAD_DIM), dtype=jnp.float32) * scale, 'Wo': jax.random.normal(k4, (N_HEAD * HEAD_DIM, C), dtype=jnp.float32) * scale}
    _L0_attn_in = _L0_attn_setup()

    def _L0_ffn_setup():
        import jax, jax.numpy as jnp
        import numpy as np
        D_MODEL = 128
        D_FF = 512
        N_EXPERTS = 8
        TOP_K = 2

        def _ffn(x, w1, b1, w2, b2):
            h = jax.nn.gelu(x @ w1.T + b1)
            return h @ w2.T + b2
        key = jax.random.key(seed)
        ks = jax.random.split(key, 12)
        s = 0.02
        x = jax.random.normal(ks[0], (4, 256, D_MODEL), dtype=jnp.float32)
        shared_w1 = jax.random.normal(ks[1], (D_FF, D_MODEL), dtype=jnp.float32) * s
        shared_b1 = jnp.zeros((D_FF,), dtype=jnp.float32)
        shared_w2 = jax.random.normal(ks[2], (D_MODEL, D_FF), dtype=jnp.float32) * s
        shared_b2 = jnp.zeros((D_MODEL,), dtype=jnp.float32)
        router_w = jax.random.normal(ks[3], (N_EXPERTS, D_MODEL), dtype=jnp.float32) * s
        router_b = jnp.zeros((N_EXPERTS,), dtype=jnp.float32)
        spec_w1 = jax.random.normal(ks[4], (N_EXPERTS, D_FF, D_MODEL), dtype=jnp.float32) * s
        spec_b1 = jnp.zeros((N_EXPERTS, D_FF), dtype=jnp.float32)
        spec_w2 = jax.random.normal(ks[5], (N_EXPERTS, D_MODEL, D_FF), dtype=jnp.float32) * s
        spec_b2 = jnp.zeros((N_EXPERTS, D_MODEL), dtype=jnp.float32)
        return dict(x=x, shared_w1=shared_w1, shared_b1=shared_b1, shared_w2=shared_w2, shared_b2=shared_b2, router_w=router_w, router_b=router_b, spec_w1=spec_w1, spec_b1=spec_b1, spec_w2=spec_w2, spec_b2=spec_b2)
    _L0_ffn_in = _L0_ffn_setup()

    def _L1_attn_setup():
        import jax, jax.numpy as jnp
        import numpy as np
        B, T, E, H = (2, 256, 128, 16)
        HD = E // H

        def _xavier(key, shape):
            limit = float(np.sqrt(6.0 / (shape[0] + shape[1])))
            return jax.random.uniform(key, shape, dtype=jnp.float32, minval=-limit, maxval=limit)
        key = jax.random.key(seed)
        kx, kq, kk, kv = jax.random.split(key, 4)
        return {'x': jax.random.normal(kx, (B, T, E), dtype=jnp.float32), 'w_Q': _xavier(kq, (E, E)), 'w_K': _xavier(kk, (E, E)), 'w_V': _xavier(kv, (E, E))}
    _L1_attn_in = _L1_attn_setup()

    def _L1_ffn_setup():
        import jax, jax.numpy as jnp
        import numpy as np
        key = jax.random.key(seed)
        ks = jax.random.split(key, 6)
        B, L, D, E = (4, 256, 128, 4)
        H = 4 * D
        x = jax.random.normal(ks[0], (B, L, D), dtype=jnp.float32)
        rW1 = jax.random.normal(ks[1], (D, 2 * D), dtype=jnp.float32) * (2.0 / D) ** 0.5
        rb1 = jnp.zeros((2 * D,), dtype=jnp.float32)
        rW2 = jax.random.normal(ks[2], (2 * D, E), dtype=jnp.float32) * (2.0 / (2 * D)) ** 0.5
        rb2 = jnp.zeros((E,), dtype=jnp.float32)
        We1 = jax.random.normal(ks[3], (E, D, H), dtype=jnp.float32) * (2.0 / D) ** 0.5
        be1 = jnp.zeros((E, H), dtype=jnp.float32)
        We2 = jax.random.normal(ks[4], (E, H, D), dtype=jnp.float32) * (2.0 / H) ** 0.5
        be2 = jnp.zeros((E, D), dtype=jnp.float32)
        return {'x': x, 'rW1': rW1, 'rb1': rb1, 'rW2': rW2, 'rb2': rb2, 'We1': We1, 'be1': be1, 'We2': We2, 'be2': be2}
    _L1_ffn_in = _L1_ffn_setup()
    _d = {'L0_attn_x': _L0_attn_in['x'], 'L0_attn_Wq': _L0_attn_in['Wq'], 'L0_attn_Wk': _L0_attn_in['Wk'], 'L0_attn_Wv': _L0_attn_in['Wv'], 'L0_attn_Wo': _L0_attn_in['Wo'], 'L0_ffn_shared_w1': _L0_ffn_in['shared_w1'], 'L0_ffn_shared_b1': _L0_ffn_in['shared_b1'], 'L0_ffn_shared_w2': _L0_ffn_in['shared_w2'], 'L0_ffn_shared_b2': _L0_ffn_in['shared_b2'], 'L0_ffn_router_w': _L0_ffn_in['router_w'], 'L0_ffn_router_b': _L0_ffn_in['router_b'], 'L0_ffn_spec_w1': _L0_ffn_in['spec_w1'], 'L0_ffn_spec_b1': _L0_ffn_in['spec_b1'], 'L0_ffn_spec_w2': _L0_ffn_in['spec_w2'], 'L0_ffn_spec_b2': _L0_ffn_in['spec_b2'], 'L1_attn_w_Q': _L1_attn_in['w_Q'], 'L1_attn_w_K': _L1_attn_in['w_K'], 'L1_attn_w_V': _L1_attn_in['w_V'], 'L1_ffn_rW1': _L1_ffn_in['rW1'], 'L1_ffn_rb1': _L1_ffn_in['rb1'], 'L1_ffn_rW2': _L1_ffn_in['rW2'], 'L1_ffn_rb2': _L1_ffn_in['rb2'], 'L1_ffn_We1': _L1_ffn_in['We1'], 'L1_ffn_be1': _L1_ffn_in['be1'], 'L1_ffn_We2': _L1_ffn_in['We2'], 'L1_ffn_be2': _L1_ffn_in['be2']}
    _x0 = _d['L0_attn_x']
    _d['L0_attn_x'] = jax.random.normal(jax.random.fold_in(jax.random.key(seed), 1), (8, 512, 128), dtype=_x0.dtype)
    del _x0
    return _d

def reference(L0_attn_x, L0_attn_Wq, L0_attn_Wk, L0_attn_Wv, L0_attn_Wo, L0_ffn_shared_w1, L0_ffn_shared_b1, L0_ffn_shared_w2, L0_ffn_shared_b2, L0_ffn_router_w, L0_ffn_router_b, L0_ffn_spec_w1, L0_ffn_spec_b1, L0_ffn_spec_w2, L0_ffn_spec_b2, L1_attn_w_Q, L1_attn_w_K, L1_attn_w_V, L1_ffn_rW1, L1_ffn_rb1, L1_ffn_rW2, L1_ffn_rb2, L1_ffn_We1, L1_ffn_be1, L1_ffn_We2, L1_ffn_be2):

    def _L0_attn_ref(x, Wq, Wk, Wv, Wo):
        import jax, jax.numpy as jnp
        import numpy as np
        import math
        N_HEAD = 16
        N_KV_HEAD = 4
        HEAD_DIM = 64
        ROPE_THETA = 10000.0

        def _rope_cache(T, D, dtype):
            inv_freq = 1.0 / ROPE_THETA ** (jnp.arange(0, D, 2, dtype=dtype) / D)
            t = jnp.arange(T, dtype=dtype)
            freqs = jnp.einsum('i,j->ij', t, inv_freq)
            return (jnp.cos(freqs)[None, None], jnp.sin(freqs)[None, None])

        def _apply_rope(x, cos, sin):
            x1 = x[..., ::2]
            x2 = x[..., 1::2]
            return jnp.concatenate([x1 * cos - x2 * sin, x1 * sin + x2 * cos], axis=-1)
        B, T, C = x.shape
        H, Hkv, D = (N_HEAD, N_KV_HEAD, HEAD_DIM)
        q = (x @ Wq).reshape(B, T, H, D).transpose(0, 2, 1, 3)
        k = (x @ Wk).reshape(B, T, Hkv, D).transpose(0, 2, 1, 3)
        v = (x @ Wv).reshape(B, T, Hkv, D).transpose(0, 2, 1, 3)
        rep = H // Hkv
        k = jnp.repeat(k, rep, axis=1)
        v = jnp.repeat(v, rep, axis=1)
        cos, sin = _rope_cache(T, D, x.dtype)
        q = _apply_rope(q, cos, sin)
        k = _apply_rope(k, cos, sin)
        att = jnp.einsum('bhtd,bhsd->bhts', q, k) / math.sqrt(D)
        mask = jnp.tril(jnp.ones((T, T), dtype=bool))
        att = jnp.where(mask, att, -jnp.inf)
        att = jax.nn.softmax(att, axis=-1)
        y = jnp.einsum('bhts,bhsd->bhtd', att, v)
        y = y.transpose(0, 2, 1, 3).reshape(B, T, H * D)
        return y @ Wo

    def _L0_ffn_ref(x, shared_w1, shared_b1, shared_w2, shared_b2, router_w, router_b, spec_w1, spec_b1, spec_w2, spec_b2):
        import jax, jax.numpy as jnp
        import numpy as np
        D_MODEL = 128
        D_FF = 512
        N_EXPERTS = 8
        TOP_K = 2

        def _ffn(x, w1, b1, w2, b2):
            h = jax.nn.gelu(x @ w1.T + b1)
            return h @ w2.T + b2
        B, T, D = x.shape
        xf = x.reshape(-1, D)
        U = xf.shape[0]
        logits = xf @ router_w.T + router_b
        routing = jax.nn.softmax(logits, axis=-1)
        sel_w, sel_idx = jax.lax.top_k(routing, TOP_K)
        sel_w = sel_w / sel_w.sum(axis=-1, keepdims=True)
        comb = jnp.zeros_like(routing).at[jnp.arange(U)[:, None], sel_idx].set(sel_w)
        shared_out = _ffn(xf, shared_w1, shared_b1, shared_w2, shared_b2)

        def body(acc, params):
            w1, b1, w2, b2, we = params
            return (acc + we[:, None] * _ffn(xf, w1, b1, w2, b2), None)
        acc0 = jnp.zeros_like(shared_out)
        acc, _ = jax.lax.scan(body, acc0, (spec_w1, spec_b1, spec_w2, spec_b2, comb.T))
        return (shared_out + acc).reshape(B, T, D)

    def _L1_attn_ref(x, w_Q, w_K, w_V):
        import jax, jax.numpy as jnp
        import numpy as np
        B, T, E, H = (2, 256, 128, 16)
        HD = E // H

        def _xavier(key, shape):
            limit = float(np.sqrt(6.0 / (shape[0] + shape[1])))
            return jax.random.uniform(key, shape, dtype=jnp.float32, minval=-limit, maxval=limit)
        Bs, Ts, Es = x.shape
        q = (x @ w_Q).reshape(Bs, Ts, H, HD).transpose(0, 2, 1, 3)
        k = (x @ w_K).reshape(Bs, Ts, H, HD).transpose(0, 2, 1, 3)
        v = (x @ w_V).reshape(Bs, Ts, H, HD).transpose(0, 2, 1, 3)
        scores = jnp.einsum('bhtd,bhsd->bhts', q, k) / jnp.sqrt(jnp.asarray(HD, x.dtype))
        probs = jax.nn.softmax(scores, axis=-1)
        attn = jnp.einsum('bhts,bhsd->bhtd', probs, v)
        return attn.transpose(0, 2, 1, 3).reshape(Bs, Ts, H * HD)

    def _L1_ffn_ref(x, rW1, rb1, rW2, rb2, We1, be1, We2, be2):
        import jax, jax.numpy as jnp
        import numpy as np
        E = We1.shape[0]
        top_k = min(2, E)
        rh = jax.nn.gelu(x @ rW1 + rb1, approximate=False)
        router_logits = rh @ rW2 + rb2
        router_probs = jax.nn.softmax(router_logits, axis=-1)
        expert_weights, expert_indices = jax.lax.top_k(router_probs, top_k)
        one_hot = jax.nn.one_hot(expert_indices, E, dtype=x.dtype)
        token_mask = one_hot.sum(axis=2)
        combine_w = (one_hot * expert_weights[..., None]).sum(axis=2)
        out = jnp.zeros_like(x)
        for e in range(E):
            xi = x * token_mask[..., e:e + 1]
            h = jax.nn.gelu(xi @ We1[e] + be1[e], approximate=False)
            yo = h @ We2[e] + be2[e]
            out = out + yo * combine_w[..., e:e + 1]
        return out
    x = L0_attn_x
    x = x + _layernorm(_L0_attn_ref(_layernorm(x, axis=-1), L0_attn_Wq, L0_attn_Wk, L0_attn_Wv, L0_attn_Wo), axis=-1)
    x = x + _layernorm(_L0_ffn_ref(_layernorm(x, axis=-1), L0_ffn_shared_w1, L0_ffn_shared_b1, L0_ffn_shared_w2, L0_ffn_shared_b2, L0_ffn_router_w, L0_ffn_router_b, L0_ffn_spec_w1, L0_ffn_spec_b1, L0_ffn_spec_w2, L0_ffn_spec_b2), axis=-1)
    x = x + _layernorm(_L1_attn_ref(_layernorm(x, axis=-1), L1_attn_w_Q, L1_attn_w_K, L1_attn_w_V), axis=-1)
    x = x + _layernorm(_L1_ffn_ref(_layernorm(x, axis=-1), L1_ffn_rW1, L1_ffn_rb1, L1_ffn_rW2, L1_ffn_rb2, L1_ffn_We1, L1_ffn_be1, L1_ffn_We2, L1_ffn_be2), axis=-1)
    return x

_drawn_inputs = setup_inputs


def setup_inputs(seed=0):
    import zlib

    import numpy as np

    out = dict(_drawn_inputs(seed))
    spreads = {'L0_ffn_shared_b1': (0.0, 0.1),
     'L0_ffn_shared_b2': (0.0, 0.1),
     'L0_ffn_router_b': (0.0, 0.1),
     'L0_ffn_spec_b1': (0.0, 0.1),
     'L0_ffn_spec_b2': (0.0, 0.1),
     'L1_ffn_rb1': (0.0, 0.1),
     'L1_ffn_rb2': (0.0, 0.1),
     'L1_ffn_be1': (0.0, 0.1),
     'L1_ffn_be2': (0.0, 0.1)}
    factors = {}
    for name, (base, spread) in spreads.items():
        noise = np.random.default_rng([zlib.crc32(name.encode()), seed]).standard_normal(out[name].shape)
        drawn = base * np.exp(spread * noise) if base else spread * noise
        out[name] = jnp.asarray(drawn.astype(out[name].dtype))
    for name, factor in factors.items():
        out[name] = (out[name] * factor).astype(out[name].dtype)
    return out
```

```python
from contextlib import ExitStack

import concourse.bass as bass
from concourse import mybir
from concourse.alu_op_type import AluOpType as ALU

ACT = mybir.ActivationFunctionType
F32 = mybir.dt.float32
F32R = mybir.dt.float32r
BF16 = mybir.dt.bfloat16
AX_X = mybir.AxisListType.X

P = 128
NSEQ, T, C = 8, 512, 128
NB = T // P
H0, KV0, D0 = 16, 4, 64
HALF = D0 // 2
NG = H0 // 4
H1, D1 = 16, 8
E0, E1 = 8, 4
FF = 512
NF = FF // P
EPS = 1e-5
BIG = 1e30
UNITS = H0 * NB
SEG = [P * (i * (i + 1) // 2) for i in range(NB)]
HEADW = P * NB * (NB + 1) // 2
TSEG = [0, 512, 1024, 896]
TBANK = [(4, 0), (5, 0), (6, 0), (5, 384)]
ROWS1 = 9 * D1
MROW = 96
SC1 = float(D1) ** -0.5
KSTACK_DMAS = 8 * 4
QSTACK_DMAS = 4 * 4


def sandwich_kernel(nc, io):
    with ExitStack() as ctx:
        base = (nc.sbuf_base + 63) // 64 * 64
        top = [base]

        def size(shape, dt):
            n = 2 if dt == BF16 else 4
            for s in shape[1:]:
                n *= s
            return (n + 31) // 32 * 32

        def sb(name, shape, dt=F32):
            t = nc.alloc_sbuf_tensor_at(name, shape, dt, offset=top[0])
            top[0] += size(shape, dt)
            return t

        def region(kib):
            at = top[0]
            top[0] += kib * 1024
            return [at, at + kib * 1024]

        def sub(reg, name, shape, dt=F32):
            t = nc.alloc_sbuf_tensor_at(name, shape, dt, offset=reg[0])
            reg[0] += size(shape, dt)
            assert reg[0] <= reg[1], name
            return t

        def sem(name):
            return ctx.enter_context(nc.semaphore(name))

        ps = ctx.enter_context(nc.psum_tensor("ps", [P, 8, 512], F32))

        wqa, wqb = sb("wqa", [P, NG, P]), sb("wqb", [P, NG, P])
        wka, wkb = sb("wka", [P, P]), sb("wkb", [P, P])
        wv0 = sb("wv0", [P, KV0 * D0])
        wo = sb("wo", [P, H0 * D0 // P, C])
        cos, sin = sb("cos", [P, T]), sb("sin", [P, T])
        ident, identb, maskb = sb("ident", [P, P]), sb("identb", [P, P], BF16), sb("maskb", [P, P], BF16)
        f0w1, f0b1 = sb("f0w1", [P, E0 + 1, FF]), sb("f0b1", [P, E0 + 1, NF])
        f0w2, f0b2 = sb("f0w2", [P, E0 + 1, NF, C]), sb("f0b2", [E0 + 1, C])
        r0w, r0b = sb("r0w", [P, E0]), sb("r0b", [P, E0])
        w1q, w1k, w1v = sb("w1q", [P, P]), sb("w1k", [P, P]), sb("w1v", [P, P])
        f1w1, f1b1 = sb("f1w1", [P, E1, FF]), sb("f1b1", [P, E1, NF])
        f1w2, f1b2 = sb("f1w2", [P, E1, NF, C]), sb("f1b2", [E1, C])
        r1w1, r1b1 = sb("r1w1", [P, 2 * P]), sb("r1b1", [P, 2])
        r1w2, r1b2 = sb("r1w2", [P, 2, E1]), sb("r1b2", [P, E1])
        ranks = sb("ranks", [P, E0])
        neghalf = sb("neghalf", [P, NB])
        x0, x1, x2, x3 = (sb(f"x{i}", [P, NB, C]) for i in range(4))
        xn = sb("xn", [P, NB, C])
        xta, xtb = sb("xta", [P, T]), sb("xtb", [P, T])
        st, mv, rstd = sb("st", [P, NB, 6]), sb("mv", [P, NB, 2]), sb("rstd", [P, NB])
        outt = sb("outt", [P, NB, C])
        r_q = region(32)
        qs = nc.alloc_sbuf_tensor_at("qs", [P, H0, T], F32R, offset=r_q[0])
        pt1 = sub(r_q, "pt1", [P, 4, 2, T])
        zt = sub(r_q, "zt", [P, 4, T])
        parts = sub(r_q, "parts", [P, 3, 2, T], BF16)
        r_k = region(16)
        ks1 = nc.alloc_sbuf_tensor_at("ks1", [P, KV0, T], F32R, offset=r_k[0])
        ks2 = nc.alloc_sbuf_tensor_at("ks2", [P, KV0, T], F32R, offset=r_k[0] + 8192)
        qd = sub(r_k, "qd", [P, H1, T], BF16)
        r_h = region(16)
        hi = nc.alloc_sbuf_tensor_at("hi", [P, 2, 2, T], F32R, offset=r_h[0])
        lo = nc.alloc_sbuf_tensor_at("lo", [P, 2, 2, T], F32R, offset=r_h[0] + 8192)
        kd = sub(r_h, "kd", [P, H1, T], BF16)
        r_t = region(16)
        yt = nc.alloc_sbuf_tensor_at("yt", [P, H0 // 2, T], F32, offset=r_t[0])
        tmp = nc.alloc_sbuf_tensor_at("tmp", [P, NB, C], F32, offset=r_t[0])
        t12 = sub(r_t, "t12", [P, 2, T])
        t34 = sub(r_t, "t34", [P, 2, T])
        r_p = region(25)
        hid = nc.alloc_sbuf_tensor_at("hid", [P, 2, NF, T], F32, offset=r_p[0])
        rh = nc.alloc_sbuf_tensor_at("rh", [P, 2, T], F32, offset=r_p[0] + 16384)
        acc = nc.alloc_sbuf_tensor_at("acc", [P, NB, C], F32, offset=r_p[0] + 20480)
        combt = nc.alloc_sbuf_tensor_at("combt", [E0 + 1, T], F32, offset=r_p[0] + 22528)
        rab = nc.alloc_sbuf_tensor_at("rab", [P, 2, 2, T], F32, offset=r_p[0])
        oab = nc.alloc_sbuf_tensor_at("oab", [P, 2, 2, T], F32, offset=r_p[0] + 8192)
        pb = sub(r_p, "pb", [P, 2, HEADW])
        ptt = sub(r_p, "ptt", [P, 3, HEADW])
        r_v = region(4)
        v0 = nc.alloc_sbuf_tensor_at("v0", [P, NB, KV0 * D0], F32, offset=r_v[0])
        res = sub(r_v, "res", [P, 2, T])
        vs = sb("vs", [P, NB, H1, 32])
        mt = sb("mt", [48, T], BF16)
        nm = sb("nm", [P, 8])
        sums, rsum = sb("sums", [P, 2, NB]), sb("rsum", [P, 2, NB])
        nm1, nm1r = sb("nm1", [P, NB, H1]), sb("nm1r", [P, NB, H1])
        nmp = sb("nmp", [P, NB, 3, H1], BF16)
        rc1 = sb("rc1", [P, NB * H1])
        rt = {k: sb("rt_" + k, [P, NB, E0 + 1]) for k in ("lg", "eq", "oh1", "msk", "ex", "comb")}
        rm = sb("rm", [P, 4, NB])
        assert top[0] <= nc.sbuf_usable_end, (top[0], nc.sbuf_usable_end)

        scratch = nc.dram_tensor("scratch", [2, 3, P, T], BF16).ap()

        s_w = sem("s_w"); s_comb1 = sem("s_comb1"); s_const = sem("s_const"); s_wscaled = sem("s_wscaled")
        NWA, NWF = 11, 16
        s_wf = sem("s_wf")
        a_in = sem("a_in"); a_krope = sem("a_krope")
        stats = {k: sem("stats_" + k) for k in ("ai", "ao", "bi", "bo", "ci", "co", "di", "do")}
        rs_ready = {k: sem("rs_" + k) for k in ("ai", "ao", "bi", "bo", "ci", "co", "di", "do")}
        xn_ready = {k: sem("xn_" + k) for k in "abcd"}
        xt_ps = {k: sem("xtps_" + k) for k in "abcd"}
        xt_ready = {k: sem("xt_" + k) for k in "abcd"}
        res_done = {k: sem("res_" + k) for k in "abcd"}
        chain = {k: sem("chain_" + k) for k in "abcd"}
        pch = {k: sem("pch_" + k) for k in "abcd"}
        a_pair_ps = sem("a_pair_ps"); a_pair_act = sem("a_pair_act"); a_pair_dve = sem("a_pair_dve")
        a_oa = sem("a_oa"); a_ob = sem("a_ob"); a_hi = sem("a_hi"); a_lo = sem("a_lo")
        a_v_ps = sem("a_v_ps"); a_v = sem("a_v")
        a_kst = sem("a_kst"); a_qst = [sem(f"a_qst{g}") for g in range(NG)]
        a_s = sem("a_s"); a_nm = sem("a_nm"); a_exp = sem("a_exp")
        a_pn = sem("a_pn"); a_tr = sem("a_tr"); a_pt_act = sem("a_pt_act"); a_pt_dve = sem("a_pt_dve")
        a_y_ps = sem("a_y_ps"); a_yt = sem("a_yt")
        a_o_ps = sem("a_o_ps")
        c_qk_ps = sem("c_qk_ps"); c_v_ps = sem("c_v_ps"); c_v = sem("c_v"); c_parts = sem("c_parts")
        c_scr = sem("c_scr"); c_stack = sem("c_stack"); c_pad = sem("c_pad")
        c_s1 = sem("c_s1"); c_nm = sem("c_nm")
        c_nmp = sem("c_nmp"); c_mt_ps = sem("c_mt_ps"); c_mt = sem("c_mt"); c_mrow = sem("c_mrow")
        c_s2 = sem("c_s2"); c_exp = sem("c_exp")
        c_pv = sem("c_pv"); c_z = sem("c_z")
        c_zt = sem("c_zt"); c_att = sem("c_att")
        f_rps = {k: sem("rps_" + k) for k in "bd"}; f_lm = {k: sem("lm_" + k) for k in "bd"}
        f_ex = {k: sem("ex_" + k) for k in "bd"}; f_comb = {k: sem("comb_" + k) for k in "bd"}
        f_ctps = {k: sem("ctps_" + k) for k in "bd"}; f_ct = {k: sem("ct_" + k) for k in "bd"}
        f_bias_ps = {k: sem("biasps_" + k) for k in "bd"}; f_bias = {k: sem("bias_" + k) for k in "bd"}
        f_h = {k: sem("h_" + k) for k in "bd"}; f_g = {k: sem("g_" + k) for k in "bd"}
        f_y = {k: sem("y_" + k) for k in "bd"}; f_acc = {k: sem("acc_" + k) for k in "bd"}
        d_rh_ps = sem("d_rh_ps"); d_rh = sem("d_rh")
        pool_dma = sem("pool_dma")

        XT = {"a": xta, "c": xtb, "b": xta, "d": xtb}
        XTBANK = {"a": 0, "c": 1, "b": 6, "d": 0}
        SRC = {"a": x0, "b": x1, "c": x2, "d": x3}
        DST = {"a": x1, "b": x2, "c": x3, "d": outt}
        FFN = {"b": dict(n=E0 + 1, routed=E0, w1=f0w1, b1=f0b1, w2=f0w2, b2=f0b2, rb=r0b),
               "d": dict(n=E1, routed=E1, w1=f1w1, b1=f1b1, w2=f1w2, b2=f1b2, rb=r1b2)}

        x_dram, out_dram = io["x"], io["out"]
        block = ctx.enter_context(nc.Block())


        @block.sync
        def _(sp):
            for n, (name, dst) in enumerate((("wka", wka), ("wkb", wkb), ("wv0", wv0), ("cos", cos), ("sin", sin),
                              ("ident", ident), ("identb", identb), ("maskb", maskb), ("wqa", wqa), ("wqb", wqb),
                              ("wo", wo), ("r0w", r0w), ("r0b", r0b), ("f0b1", f0b1), ("f0b2", f0b2),
                              ("f0w1", f0w1), ("f0w2", f0w2), ("w1q", w1q), ("w1k", w1k), ("w1v", w1v),
                              ("r1w1", r1w1), ("r1b1", r1b1), ("r1w2", r1w2),
                              ("f1b1", f1b1), ("f1b2", f1b2), ("f1w1", f1w1), ("f1w2", f1w2))):
                if n == 0:
                    sp.dma_start(x0[:], x_dram[0]).then_inc(a_in, 16)
                sp.dma_start(dst[:], io[name]).then_inc(s_w if n < NWA else s_wf, 16)

            def a_main(b):
                if not isinstance(b, int):
                    sp.wait_ge(res_done["a"], b)
                    sp.dma_start(x0[:], x_dram[b]).then_inc(a_in, 16)
                for p in range(1 + NG):
                    sp.wait_ge(a_hi, 5 * b + p + 1)
                    sp.wait_ge(a_lo, 5 * b + p + 1)
                    for h in range(4):
                        rows = slice(HALF * h, HALF * h + HALF)
                        a, bb = hi[rows, p % 2, 0, :], hi[rows, p % 2, 1, :]
                        la, lb = lo[rows, p % 2, 0, :], lo[rows, p % 2, 1, :]
                        if p == 0:
                            for dst, order in ((ks1, (a, bb, la, lb)), (ks2, (la, lb, a, bb))):
                                for r, src in enumerate(order):
                                    sp.dma_start(dst[HALF * r:HALF * r + HALF, h, :].bitcast(F32),
                                                 src.bitcast(F32)).then_inc(a_kst, 16)
                        else:
                            for r, src in enumerate((a, bb, la, lb)):
                                sp.dma_start(qs[HALF * r:HALF * r + HALF, 4 * (p - 1) + h, :].bitcast(F32),
                                             src.bitcast(F32)).then_inc(a_qst[p - 1], 16)

            def c_main(b):
                sp.wait_ge(c_parts, b + 1)
                for w in range(2):
                    sp.dma_start(scratch[w].rearrange("s p t -> p s t"), parts[:, :, w, :]).then_inc(c_scr, 16)
                sp.wait_ge(c_scr, 32 * b + 32)
                sp.wait_ge(c_pad, 3 * b + 3)
                for s in range(3):
                    for s2 in range(3):
                        r = (3 * s + s2) * D1
                        sp.dma_start(qd[r:r + D1, :, :],
                                     scratch[0, s].rearrange("(h d) t -> d h t", d=D1)).then_inc(c_stack, 16)
                        sp.dma_start(kd[r:r + D1, :, :],
                                     scratch[1, s2].rearrange("(h d) t -> d h t", d=D1)).then_inc(c_stack, 16)
                sp.wait_ge(c_mt, b + 1)
                for s in range(3):
                    sp.dma_start(qd[MROW + s:MROW + s + 1, :, :], mt[16 * s:16 * s + 16, :]).then_inc(c_mrow, 16)

            a_main(0)
            with sp.Fori(1, NSEQ) as i:
                a_main(i)
                c_main(i - 1)
            c_main(NSEQ - 1)

        @block.gpsimd
        def _(pool):
            pool.memset(neghalf[:], -0.5).then_inc(s_const, 1)
            pool.memset(vs[:], 0.0).then_inc(s_const, 1)
            pool.dma_start(r1b2[:], io["r1b2"]).then_inc(pool_dma, 16)
            pool.wait_ge(s_const, 2)
            pool.memset(vs[:, :, :, D1:D1 + 1], 1.0).then_inc(s_const, 1)
            for e in range(E0):
                pool.memset(ranks[:, e:e + 1], float(E0 - e)).then_inc(s_const, 1)
            pool.wait_ge(s_const, 3 + E0)

            def norm_scale(k, which, b, n):
                pool.wait_ge(stats[which], b + 1)
                pool.nop(nofuse=True)
                pool.tensor_scalar(rstd[:], mv[:, :, 1], EPS, None, ALU.add).then_inc(pch[k], 1)
                pool.wait_ge(pch[k], PCH[k] * b + n)
                pool.tensor_tensor(rstd[:], rstd[:], neghalf[:], ALU.pow).then_inc(rs_ready[which], 1)

            PCH = {"a": 2 + 5, "b": 2, "c": 2, "d": 2}

            def a_main(b):
                for p in range(1 + NG):
                    pool.wait_ge(a_pair_act, 5 * b + p + 1)
                    if p == 0:
                        if isinstance(b, int):
                            pool.wait_ge(s_w, 16 * NWA)
                    else:
                        pool.wait_ge(a_ob, 5 * b + p)
                    pool.tensor_tensor(t34[:, 0, :], rab[:, p % 2, 0, :], sin[:], ALU.mult)
                    pool.tensor_tensor(t34[:, 1, :], rab[:, p % 2, 1, :], cos[:], ALU.mult).then_inc(pch["a"], 1)
                    pool.wait_ge(pch["a"], PCH["a"] * b + 1 + p + 1)
                    if p > 1:
                        pool.wait_ge(a_hi, 5 * b + p - 1)
                        pool.wait_ge(a_lo, 5 * b + p - 1)
                    pool.tensor_tensor(oab[:, p % 2, 1, :], t34[:, 0, :], t34[:, 1, :], ALU.add).then_inc(a_ob, 1)

            def c_in(b):
                norm_scale("c", "ci", b, 1)
                pool.wait_ge(xt_ready["c"], b + 1)
                pool.nop(nofuse=True)
                pool.memset(qd[64:P, :, :].bitcast(F32), 0.0).then_inc(c_pad, 1)
                pool.wait_ge(c_pad, 3 * b + 1)
                pool.nop(nofuse=True)
                pool.memset(kd[64:MROW, :, :].bitcast(F32), 0.0).then_inc(c_pad, 1)
                pool.wait_ge(c_pad, 3 * b + 2)
                pool.nop(nofuse=True)
                pool.memset(kd[MROW:P, :, :], 1.0).then_inc(c_pad, 1)
                pool.wait_ge(c_pad, 3 * b + 3)
                pool.nop(nofuse=True)

            def d_out(b):
                norm_scale("d", "do", b, 2)
                pool.wait_ge(res_done["d"], b + 1)
                pool.dma_start(out_dram[b], outt[:]).then_inc(pool_dma, 16)

            norm_scale("a", "ai", 0, 1)
            a_main(0)
            norm_scale("a", "ao", 0, 2 + 5)
            norm_scale("b", "bi", 0, 1)
            norm_scale("b", "bo", 0, 2)
            with pool.Fori(1, NSEQ) as i:
                norm_scale("a", "ai", i, 1)
                a_main(i)
                c_in(i - 1)
                norm_scale("a", "ao", i, 2 + 5)
                norm_scale("b", "bi", i, 1)
                norm_scale("c", "co", i - 1, 2)
                norm_scale("d", "di", i - 1, 1)
                norm_scale("b", "bo", i, 2)
                d_out(i - 1)
            c_in(NSEQ - 1)
            norm_scale("c", "co", NSEQ - 1, 2)
            norm_scale("d", "di", NSEQ - 1, 1)
            d_out(NSEQ - 1)
            pool.wait_ge(pool_dma, 16 * (NSEQ + 1))

        @block.tensor
        def _(pe):
            def to_channels(k, b):
                pe.wait_ge(xn_ready[k], b + 1)
                if k == "a" and isinstance(b, int):
                    pe.wait_ge(s_w, 16 * NWA)
                for t in range(NB):
                    last = pe.transpose(ps[:, XTBANK[k], t * P:t * P + P], xn[:, t, :], ident[:])
                last.then_inc(xt_ps[k], 1)

            def a_main(b):
                pe.wait_ge(xt_ready["a"], b + 1)
                for p in range(1 + NG):
                    if p >= 2:
                        pe.wait_ge(a_pair_act, 5 * b + p - 1)
                    if p == 1 and isinstance(b, int):
                        pe.wait_ge(s_wscaled, 2)
                    wa = wka[:] if p == 0 else wqa[:, p - 1, :]
                    wb = wkb[:] if p == 0 else wqb[:, p - 1, :]
                    bank = 2 + 2 * (p % 2)
                    pe.matmul(ps[:, bank, :], wa, xta[:], start=True, stop=True)
                    pe.matmul(ps[:, bank + 1, :], wb, xta[:], start=True, stop=True).then_inc(a_pair_ps, 1)
                    if p == 1:
                        for t in range(NB):
                            last = pe.matmul(ps[:, 6 + t // 2, 256 * (t % 2):256 * (t % 2) + 256],
                                             xta[:, t * P:t * P + P], wv0[:], start=True, stop=True)
                        last.then_inc(a_v_ps, 1)
                pe.wait_ge(a_pair_act, 5 * b + 5)
                pe.wait_ge(a_v, b + 1)
                pe.wait_ge(a_kst, 16 * KSTACK_DMAS * b + 16 * KSTACK_DMAS)

                def scores(h):
                    if h % 4 == 0:
                        pe.wait_ge(a_qst[h // 4], 16 * QSTACK_DMAS * b + 16 * QSTACK_DMAS)
                    for i in range(NB):
                        u = NB * h + i
                        n = P * (i + 1)
                        if u >= 4:
                            pe.wait_ge(a_exp, UNITS * b + u - 3)
                        q = qs[:, h, P * i:P * i + P]
                        s = ps[:, u % 4, 0:n]
                        pe.matmul(ps[:, u % 4, n - P:n], identb[:], maskb[:], start=True, stop=False,
                                  skip_group_check=True)
                        pe.matmul(s, q, ks1[:, h // 4, 0:n], start=False, stop=False, skip_group_check=True)
                        pe.matmul(s, q, ks2[:, h // 4, 0:n], start=False, stop=True,
                                  skip_group_check=True).then_inc(a_s, 1)

                def transposes(h):
                    pe.wait_ge(a_pn, H0 * b + h + 1)
                    if h > 0:
                        pe.wait_ge(a_pt_act, H0 * b + h)
                        pe.wait_ge(a_pt_dve, H0 * b + h)
                    for i in range(NB):
                        for kb in range(i + 1):
                            bank, col = TBANK[kb]
                            col += P * (i - kb)
                            last = pe.transpose(ps[:, bank, col:col + P],
                                                pb[:, h % 2, SEG[i] + P * kb:SEG[i] + P * kb + P], ident[:])
                    last.then_inc(a_tr, 1)

                def weighted_values(j):
                    pe.wait_ge(a_pt_act, H0 * b + 2 * j + 2)
                    pe.wait_ge(a_pt_dve, H0 * b + 2 * j + 2)
                    if j > 0:
                        pe.wait_ge(a_yt, (H0 // 2) * b + j)
                    kv = j // 2
                    for kb in range(NB):
                        for s in range(2):
                            n = T - P * kb
                            last = pe.matmul(ps[64 * s:64 * s + 64, 7, P * kb:T],
                                             v0[:, kb, D0 * kv:D0 * kv + D0],
                                             ptt[:, (2 * j + s) % 3, TSEG[kb]:TSEG[kb] + n],
                                             start=(kb == 0), stop=(kb == NB - 1), skip_group_check=True)
                    last.then_inc(a_y_ps, 1)

                for s in range(H0 + 2):
                    if s < H0:
                        scores(s)
                    if 1 <= s <= H0:
                        transposes(s - 1)
                    if s >= 3 and s % 2:
                        weighted_values((s - 3) // 2)

            def a_out(b):
                pe.wait_ge(a_yt, (H0 // 2) * b + H0 // 2)
                for t in range(NB):
                    for j in range(H0 // 2):
                        last = pe.matmul(ps[:, 0, t * P:t * P + P], yt[:, j, t * P:t * P + P], wo[:, j, :],
                                         start=(j == 0), stop=(j == H0 // 2 - 1))
                last.then_inc(a_o_ps, 1)

            def c_main(b):
                pe.wait_ge(xt_ready["c"], b + 1)
                pe.matmul(ps[:, 2, :], w1q[:], xtb[:], start=True, stop=True)
                pe.matmul(ps[:, 3, :], w1k[:], xtb[:], start=True, stop=True).then_inc(c_qk_ps, 1)
                for t in range(NB):
                    last = pe.matmul(ps[:, 4, t * P:t * P + P], xtb[:, t * P:t * P + P], w1v[:],
                                     start=True, stop=True)
                last.then_inc(c_v_ps, 1)
                pe.wait_ge(c_v, b + 1)
                pe.wait_ge(c_stack, 16 * 18 * b + 16 * 18)
                for v in range(32):
                    i, hp = v // 8, v % 8
                    if v >= 3:
                        pe.wait_ge(c_nm, 32 * b + v - 2)
                    for g in range(2):
                        last = pe.matmul(ps[:, 2 + 2 * (v % 3) + g, :], qd[:, 2 * hp + g, i * P:i * P + P],
                                         kd[:, 2 * hp + g, :], start=True, stop=True)
                    last.then_inc(c_s1, 1)
                pe.wait_ge(c_nmp, b + 1)
                pe.nop(nofuse=True)
                mtp = ps[0:48, 0, 0:T // 2].bitcast(BF16)
                for t in range(NB):
                    last = pe.transpose(mtp[:, t * P:t * P + P],
                                        nmp[:, t, :, :].rearrange("p s h -> p (s h)"), identb[:])
                last.then_inc(c_mt_ps, 1)
                pe.wait_ge(c_mrow, 48 * b + 48)

                def scores(w):
                    hg, kb, gp = w // 8, (w // 2) % 4, w % 2
                    if w >= 3:
                        pe.wait_ge(c_exp, 32 * b + w - 2)
                    for g in range(2):
                        h = 4 * hg + 2 * gp + g
                        last = pe.matmul(ps[:, 2 + 2 * (w % 3) + g, :], kd[:, h, kb * P:kb * P + P], qd[:, h, :],
                                         start=True, stop=True)
                    last.then_inc(c_s2, 1)

                def weighted_values(y):
                    hg, kb = y // 4, y % 4
                    pe.wait_ge(c_exp, 32 * b + 2 * y + 2)
                    if kb == 0 and hg >= 2:
                        pe.wait_ge(c_z, 4 * b + hg - 1)
                    for g in range(4):
                        last = pe.matmul(ps[32 * g:32 * g + 32, hg % 2, :], vs[:, kb, 4 * hg + g, :],
                                         pt1[:, (2 * y + g // 2) % 4, g % 2, :],
                                         start=(kb == 0), stop=(kb == NB - 1), skip_group_check=True)
                    last.then_inc(c_pv, 1)

                for y in range(16 + 1):
                    if y < 16:
                        scores(2 * y)
                        scores(2 * y + 1)
                    if y >= 1:
                        weighted_values(y - 1)

            def c_out(b):
                pe.wait_ge(c_z, 4 * b + 4)
                for i in range(NB):
                    for hg in range(4):
                        last = pe.transpose(ps[:, 2 + i, hg * P:hg * P + P], zt[:, hg, i * P:i * P + P], ident[:])
                last.then_inc(c_zt, 1)

            def experts(k, b):
                g = FFN[k]
                n, xt = g["n"], XT[k]

                def up(e):
                    for f in range(NF):
                        u = NF * e + f
                        if u >= 4:
                            pe.wait_ge(f_g[k], NF * n * b + u - 3)
                        pe.matmul(ps[:, 2 + u % 4, :], g["w1"][:, e, f * P:f * P + P], xt[:],
                                  start=True, stop=True).then_inc(f_h[k], 1)

                def down(e):
                    pe.wait_ge(f_g[k], NF * n * b + NF * e + NF)
                    if e >= 2:
                        pe.wait_ge(f_acc[k], n * b + e - 1)
                    for t in range(NB):
                        for f in range(NF):
                            last = pe.matmul(ps[:, 6 + e % 2, t * P:t * P + P], hid[:, e % 2, f, t * P:t * P + P],
                                             g["w2"][:, e, f, :], start=(f == 0), stop=(f == NF - 1))
                    last.then_inc(f_y[k], 1)

                def weighted_bias():
                    pe.wait_ge(f_comb[k], b + 1)
                    for t in range(NB):
                        last = pe.transpose(ps[0:n, 1, t * P:t * P + P], rt["comb"][:, t, 0:n], ident[:])
                    last.then_inc(f_ctps[k], 1)
                    pe.wait_ge(f_ct[k], b + 1)
                    for t in range(NB):
                        last = pe.matmul(ps[:, 1, t * P:t * P + P], combt[0:n, t * P:t * P + P], g["b2"][0:n, :],
                                         start=True, stop=True)
                    last.then_inc(f_bias_ps[k], 1)

                up(0)
                up(1)
                weighted_bias()
                for e in range(n):
                    down(e)
                    if e + 2 < n:
                        up(e + 2)

            def b_main(b):
                pe.wait_ge(xt_ready["b"], b + 1)
                if isinstance(b, int):
                    pe.wait_ge(s_wf, 16 * NWF)
                for t in range(NB):
                    last = pe.matmul(ps[:, 1, t * E0:t * E0 + E0], xta[:, t * P:t * P + P], r0w[:],
                                     start=True, stop=True)
                last.then_inc(f_rps["b"], 1)
                if not isinstance(b, int):
                    pe.wait_ge(c_att, (b - 1) + 1)
                experts("b", b)

            def d_main(b):
                pe.wait_ge(xt_ready["d"], b + 1)
                pe.wait_ge(c_att, b + 1)
                for f in range(2):
                    pe.matmul(ps[:, 2 + f, :], r1w1[:, f * P:f * P + P], xtb[:], start=True,
                              stop=True).then_inc(d_rh_ps, 1)
                pe.wait_ge(d_rh, 2 * b + 2)
                for t in range(NB):
                    for f in range(2):
                        last = pe.matmul(ps[:, 1, t * E1:t * E1 + E1], rh[:, f, t * P:t * P + P], r1w2[:, f, :],
                                         start=(f == 0), stop=(f == 1))
                last.then_inc(f_rps["d"], 1)
                experts("d", b)

            to_channels("a", 0)
            a_main(0)
            a_out(0)
            to_channels("b", 0)
            b_main(0)
            with pe.Fori(1, NSEQ) as i:
                to_channels("a", i)
                a_main(i)
                to_channels("c", i - 1)
                a_out(i)
                c_main(i - 1)
                to_channels("b", i)
                c_out(i - 1)
                b_main(i)
                to_channels("d", i - 1)
                d_main(i - 1)
            to_channels("c", NSEQ - 1)
            c_main(NSEQ - 1)
            c_out(NSEQ - 1)
            to_channels("d", NSEQ - 1)
            d_main(NSEQ - 1)

        @block.scalar
        def _(act):
            act.wait_ge(s_w, 16 * NWA)
            act.activation(wqa[:], wqa[:], ACT.Copy, scale=float(D0) ** -0.5).then_inc(s_wscaled, 1)
            act.activation(wqb[:], wqb[:], ACT.Copy, scale=float(D0) ** -0.5).then_inc(s_wscaled, 1)

            def copy_channels(k, b):
                act.wait_ge(xt_ps[k], b + 1)
                act.activation(XT[k][:], ps[:, XTBANK[k], :], ACT.Copy).then_inc(xt_ready[k], 1)

            def a_main(b):
                def take_pair(p):
                    act.wait_ge(a_pair_ps, 5 * b + p + 1)
                    if p >= 2:
                        act.wait_ge(a_ob, 5 * b + p - 1)
                        act.wait_ge(a_oa, 5 * b + p - 1)
                    bank = 2 + 2 * (p % 2)
                    act.activation(rab[:, p % 2], ps[:, bank:bank + 2, :], ACT.Copy).then_inc(a_pair_act, 1)

                def high(p):
                    act.wait_ge(a_oa, 5 * b + p + 1)
                    act.wait_ge(a_ob, 5 * b + p + 1)
                    if p >= 2:
                        if p == 2:
                            act.wait_ge(a_kst, 16 * KSTACK_DMAS * b + 16 * KSTACK_DMAS)
                        else:
                            act.wait_ge(a_qst[p - 3], 16 * QSTACK_DMAS * b + 16 * QSTACK_DMAS)
                    act.activation(hi[:, p % 2], oab[:, p % 2], ACT.Copy).then_inc(a_hi, 1)

                for p in range(1 + NG + 1):
                    if p <= NG:
                        take_pair(p)
                    if p == 1:
                        act.wait_ge(a_v_ps, b + 1)
                        act.activation(v0[:].rearrange("p t c -> p (t c)").rearrange("p (a c) -> p a c", a=2),
                                       ps[:, 6:8, :], ACT.Copy).then_inc(a_v, 1)
                    if p >= 1:
                        high(p - 1)

                def softmax(h):
                    for i in range(NB):
                        u = NB * h + i
                        n = P * (i + 1)
                        act.wait_ge(a_nm, UNITS * b + u + 1)
                        if i == 0 and h >= 2:
                            act.wait_ge(a_tr, H0 * b + h - 1)
                        act.activation(pb[:, h % 2, SEG[i]:SEG[i] + n], ps[:, u % 4, 0:n], ACT.Exp,
                                       bias=nm[:, u % 8:u % 8 + 1],
                                       accum_out=sums[:, h % 2, i:i + 1]).then_inc(a_exp, 1)

                for s in range(H0 + 2):
                    if s < H0:
                        softmax(s)
                    if 1 <= s <= H0:
                        h = s - 1
                        act.wait_ge(a_tr, H0 * b + h + 1)
                        if h >= 3:
                            act.wait_ge(a_y_ps, (H0 // 2) * b + (h - 3) // 2 + 1)
                        act.activation(ptt[:, h % 3, 512:HEADW],
                                       ps[:, 5:7, :].rearrange("p a c -> p (a c)")[:, 0:768],
                                       ACT.Copy).then_inc(a_pt_act, 1)
                    if s >= 3 and s % 2:
                        j = (s - 3) // 2
                        act.wait_ge(a_y_ps, (H0 // 2) * b + j + 1)
                        act.activation(yt[:, j, :], ps[:, 7, :], ACT.Copy).then_inc(a_yt, 1)

            def c_main(b):
                act.wait_ge(c_v_ps, b + 1)
                act.activation(vs[:, :, :, 0:D1].rearrange("p t h d -> p (t h) d"),
                               ps[:, 4, :].rearrange("p (t d) -> p t d", d=D1), ACT.Copy).then_inc(c_v, 1)
                act.wait_ge(c_mt_ps, b + 1)
                act.activation(mt[:], ps[0:48, 0, 0:T // 2].bitcast(BF16), ACT.Copy).then_inc(c_mt, 1)
                for w in range(32):
                    act.wait_ge(c_s2, 32 * b + w + 1)
                    if w >= 4:
                        act.wait_ge(c_pv, 16 * b + (w - 4) // 2 + 1)
                    bank = 2 + 2 * (w % 3)
                    act.activation(pt1[:, w % 4], ps[:, bank:bank + 2, :], ACT.Exp, scale=SC1).then_inc(c_exp, 1)

            def experts(k, b, gelu):
                g = FFN[k]
                n, r = g["n"], g["routed"]
                act.wait_ge(f_lm[k], b + 1)
                act.activation(rt["ex"][:, :, 0:r], rt["lg"][:, :, 0:r], ACT.Exp).then_inc(f_ex[k], 1)
                for e in range(n):
                    for f in range(NF):
                        u = NF * e + f
                        act.wait_ge(f_h[k], NF * n * b + u + 1)
                        if f == 0 and e >= 2:
                            act.wait_ge(f_y[k], n * b + e - 1)
                        act.activation(hid[:, e % 2, f, :], ps[:, 2 + u % 4, :], gelu,
                                       bias=g["b1"][:, e, f:f + 1]).then_inc(f_g[k], 1)
                    if e == 0:
                        act.wait_ge(f_ctps[k], b + 1)
                        act.activation(combt[0:n, :], ps[0:n, 1, :], ACT.Copy).then_inc(f_ct[k], 1)

            def d_main(b):
                for f in range(2):
                    act.wait_ge(d_rh_ps, 2 * b + f + 1)
                    act.activation(rh[:, f, :], ps[:, 2 + f, :], ACT.Gelu, bias=r1b1[:, f:f + 1]).then_inc(d_rh, 1)
                experts("d", b, ACT.Gelu)

            def b_main(b):
                if isinstance(b, int):
                    act.wait_ge(s_wf, 16 * NWF)
                experts("b", b, ACT.Gelu_apprx_tanh)

            copy_channels("a", 0)
            a_main(0)
            copy_channels("b", 0)
            b_main(0)
            with act.Fori(1, NSEQ) as i:
                copy_channels("a", i)
                a_main(i)
                copy_channels("c", i - 1)
                c_main(i - 1)
                copy_channels("b", i)
                b_main(i)
                copy_channels("d", i - 1)
                d_main(i - 1)
            copy_channels("c", NSEQ - 1)
            c_main(NSEQ - 1)
            copy_channels("d", NSEQ - 1)
            d_main(NSEQ - 1)

        @block.vector
        def _(dve):
            CH = {"a": 1 + H0 + 2, "b": 1 + 15 + 2, "c": 1 + 6 + 1 + 2, "d": 1 + 15 + 2}
            done = {}

            def link(k, b, ins):
                done[k] += 1
                ins.then_inc(chain[k], 1)
                dve.wait_ge(chain[k], CH[k] * b + done[k])

            def norm_stats(k, which, b, src):
                for t in range(NB):
                    last = dve.bn_stats(st[:, t, :], src(t))
                link(k, b, last)
                dve.nop(nofuse=True)
                for t in range(NB):
                    last = dve.bn_aggr(mv[:, t, :], st[:, t, :])
                last.then_inc(stats[which], 1)
                dve.wait_ge(rs_ready[which], b + 1)

            def norm_in(k, b):
                done[k] = 0
                if k == "a":
                    dve.wait_ge(a_in, 16 * b + 16)
                else:
                    dve.wait_ge(res_done["abcd"["abcd".index(k) - 1]], b + 1)
                norm_stats(k, k + "i", b, lambda t: SRC[k][:, t, :])
                for t in range(NB):
                    last = dve.tensor_scalar(xn[:, t, :], SRC[k][:, t, :], mv[:, t, 0:1], rstd[:, t:t + 1],
                                             ALU.subtract, ALU.mult)
                last.then_inc(xn_ready[k], 1)

            def norm_out(k, b, src):
                norm_stats(k, k + "o", b, src)
                for t in range(NB):
                    last = dve.tensor_scalar(tmp[:, t, :], src(t), mv[:, t, 0:1], rstd[:, t:t + 1],
                                             ALU.subtract, ALU.mult)
                link(k, b, last)
                if k == "d":
                    dve.wait_ge(pool_dma, 16 * b + 16)
                dve.tensor_tensor(DST[k][:], SRC[k][:], tmp[:], ALU.add).then_inc(res_done[k], 1)
                assert done[k] == CH[k], (k, done[k])

            def a_main(b):
                def rotate(p):
                    if p == 0 and isinstance(b, int):
                        dve.wait_ge(s_w, 16 * NWA)
                    dve.wait_ge(a_pair_act, 5 * b + p + 1)
                    if p > 0:
                        dve.wait_ge(a_oa, 5 * b + p)
                    dve.tensor_tensor(t12[:, 0, :], rab[:, p % 2, 0, :], cos[:], ALU.mult)
                    last = dve.tensor_tensor(t12[:, 1, :], rab[:, p % 2, 1, :], sin[:], ALU.mult)
                    last.then_inc(a_pair_dve, 1)
                    dve.wait_ge(a_pair_dve, 5 * b + p + 1)
                    if p >= 2:
                        dve.wait_ge(a_hi, 5 * b + p - 1)
                        dve.wait_ge(a_lo, 5 * b + p - 1)
                    dve.tensor_tensor(oab[:, p % 2, 0, :], t12[:, 0, :], t12[:, 1, :],
                                      ALU.subtract).then_inc(a_oa, 1)

                def low(p):
                    dve.wait_ge(a_hi, 5 * b + p + 1)
                    if p >= 2:
                        if p == 2:
                            dve.wait_ge(a_kst, 16 * KSTACK_DMAS * b + 16 * KSTACK_DMAS)
                        else:
                            dve.wait_ge(a_qst[p - 3], 16 * QSTACK_DMAS * b + 16 * QSTACK_DMAS)
                    dve.tensor_tensor(lo[:, p % 2], oab[:, p % 2], hi[:, p % 2].bitcast(F32),
                                      ALU.subtract).then_inc(a_lo, 1)

                for p in range(1 + NG + 1):
                    if p <= NG:
                        rotate(p)
                    if p >= 1:
                        low(p - 1)

                for s in range(H0 + 1):
                    if s < H0:
                        for i in range(NB):
                            u = NB * s + i
                            dve.wait_ge(a_s, UNITS * b + u + 1)
                            dve.tensor_reduce(nm[:, u % 8:u % 8 + 1], ps[:, u % 4, 0:P * (i + 1)], AX_X, ALU.max,
                                              negate=True).then_inc(a_nm, 1)
                    if s >= 1:
                        h = s - 1
                        dve.wait_ge(a_tr, H0 * b + h + 1)
                        if h >= 3:
                            dve.wait_ge(a_y_ps, (H0 // 2) * b + (h - 3) // 2 + 1)
                        dve.tensor_copy(ptt[:, h % 3, 0:512], ps[:, 4, :]).then_inc(a_pt_dve, 1)
                    if s < H0:
                        dve.wait_ge(a_exp, UNITS * b + NB * s + NB)
                        link("a", b, dve.reciprocal(rsum[:, s % 2, :], sums[:, s % 2, :]))
                        for i in range(NB):
                            seg = pb[:, s % 2, SEG[i]:SEG[i] + P * (i + 1)]
                            last = dve.tensor_scalar(seg, seg, rsum[:, s % 2, i:i + 1], None, ALU.mult)
                        last.then_inc(a_pn, 1)

            def a_out(b):
                dve.wait_ge(a_o_ps, b + 1)
                norm_out("a", b, lambda t: ps[:, 0, t * P:t * P + P])

            def c_main(b):
                dve.wait_ge(c_qk_ps, b + 1)
                qk = ps[:, 2:4, :]
                link("c", b, dve.tensor_copy(parts[:, 0], qk))
                link("c", b, dve.tensor_tensor(res[:], qk, parts[:, 0], ALU.subtract))
                link("c", b, dve.tensor_copy(parts[:, 1], res[:]))
                dve.tensor_tensor(parts[:, 2], res[:], parts[:, 1], ALU.subtract).then_inc(c_parts, 1)
                for v in range(32):
                    i, hp = v // 8, v % 8
                    bank = 2 + 2 * (v % 3)
                    dve.wait_ge(c_s1, 32 * b + v + 1)
                    dve.tensor_reduce(nm1[:, i, 2 * hp:2 * hp + 2], ps[:, bank:bank + 2, :], AX_X, ALU.max,
                                      negate=True).then_inc(c_nm, 1)
                dve.wait_ge(c_nm, 32 * b + 32)
                link("c", b, dve.tensor_copy(nmp[:, :, 0, :], nm1[:]))
                link("c", b, dve.tensor_tensor(nm1r[:], nm1[:], nmp[:, :, 0, :], ALU.subtract))
                link("c", b, dve.tensor_copy(nmp[:, :, 1, :], nm1r[:]))
                dve.tensor_tensor(nmp[:, :, 2, :], nm1r[:], nmp[:, :, 1, :], ALU.subtract).then_inc(c_nmp, 1)
                for hg in range(4):
                    dve.wait_ge(c_pv, 16 * b + 4 * hg + 4)
                    dve.tensor_copy(zt[:, hg, :], ps[:, hg % 2, :]).then_inc(c_z, 1)

            def c_out(b):
                dve.wait_ge(c_zt, b + 1)
                z = ps[:, 2:6, :].rearrange("p b c -> p (b c)").rearrange("p (n d) -> p n d", d=32)
                link("c", b, dve.reciprocal(rc1[:], z[:, :, D1]))
                att = zt[:, 0, :]
                dve.tensor_tensor(att.rearrange("p (n d) -> p n d", d=D1), z[:, :, 0:D1],
                                  rc1[:].unsqueeze(2).broadcast_to([P, NB * H1, D1]), ALU.mult).then_inc(c_att, 1)
                dve.wait_ge(c_att, b + 1)
                norm_out("c", b, lambda t: att[:, t * P:t * P + P])

            def experts(k, b):
                g = FFN[k]
                n, r = g["n"], g["routed"]
                lg, eq, oh1, msk, ex, comb = (rt[x][:, :, 0:r] for x in ("lg", "eq", "oh1", "msk", "ex", "comb"))
                rk = ranks[:, 0:r].unsqueeze(1).broadcast_to([P, NB, r])

                def wide(j):
                    return rm[:, j, :].unsqueeze(2).broadcast_to([P, NB, r])

                dve.wait_ge(f_rps[k], b + 1)
                link(k, b, dve.tensor_tensor(lg, ps[:, 1, 0:NB * r].rearrange("p (t e) -> p t e", e=r),
                                             g["rb"][:].unsqueeze(1).broadcast_to([P, NB, r]), ALU.add))
                link(k, b, dve.tensor_reduce(rm[:, 0, :], lg, AX_X, ALU.max))
                link(k, b, dve.tensor_tensor(lg, lg, wide(0), ALU.subtract))
                last = dve.scalar_tensor_tensor(out=eq, in0=lg, scalar=0.0, in1=rk, op0=ALU.is_ge, op1=ALU.mult)
                last.then_inc(f_lm[k], 1)
                dve.wait_ge(f_lm[k], b + 1)
                link(k, b, dve.tensor_reduce(rm[:, 1, :], eq, AX_X, ALU.max))
                link(k, b, dve.tensor_tensor(oh1, eq, wide(1), ALU.is_equal))
                link(k, b, dve.scalar_tensor_tensor(out=msk, in0=oh1, scalar=-BIG, in1=lg,
                                                    op0=ALU.mult, op1=ALU.add))
                link(k, b, dve.tensor_reduce(rm[:, 2, :], msk, AX_X, ALU.max))
                link(k, b, dve.tensor_tensor(eq, msk, wide(2), ALU.is_ge))
                link(k, b, dve.tensor_tensor(eq, eq, rk, ALU.mult))
                link(k, b, dve.tensor_reduce(rm[:, 3, :], eq, AX_X, ALU.max))
                link(k, b, dve.tensor_tensor(msk, eq, wide(3), ALU.is_equal))
                link(k, b, dve.tensor_tensor(msk, msk, oh1, ALU.add))
                dve.wait_ge(f_ex[k], b + 1)
                link(k, b, dve.tensor_tensor(msk, msk, ex, ALU.mult))
                link(k, b, dve.tensor_reduce(rm[:, 0, :], msk if k == "b" else ex, AX_X, ALU.add))
                link(k, b, dve.reciprocal(rm[:, 1, :], rm[:, 0, :]))
                dve.tensor_tensor(comb, msk, wide(1), ALU.mult).then_inc(f_comb[k], 1)
                dve.wait_ge(f_comb[k], b + 1)
                dve.wait_ge(f_bias_ps[k], b + 1)
                dve.tensor_copy(acc[:].rearrange("p t c -> p (t c)"), ps[:, 1, :]).then_inc(f_bias[k], 1)
                dve.wait_ge(f_bias[k], b + 1)
                for e in range(n):
                    dve.wait_ge(f_y[k], n * b + e + 1)
                    if e > 0:
                        dve.wait_ge(f_acc[k], n * b + e)
                    for t in range(NB):
                        last = dve.scalar_tensor_tensor(out=acc[:, t, :], in0=ps[:, 6 + e % 2, t * P:t * P + P],
                                                        scalar=rt["comb"][:, t, e:e + 1], in1=acc[:, t, :],
                                                        op0=ALU.mult, op1=ALU.add)
                    last.then_inc(f_acc[k], 1)

            def experts_out(k, b):
                dve.wait_ge(f_acc[k], FFN[k]["n"] * b + FFN[k]["n"])
                norm_out(k, b, lambda t: acc[:, t, :])

            def b_main(b):
                if isinstance(b, int):
                    dve.wait_ge(s_wf, 16 * NWF)
                experts("b", b)

            dve.memset(rt["comb"][:, :, E0:E0 + 1], 1.0).then_inc(s_comb1, 1)
            dve.wait_ge(s_comb1, 1)
            dve.wait_ge(s_const, 3 + E0)
            dve.wait_ge(pool_dma, 16)
            norm_in("a", 0)
            a_main(0)
            a_out(0)
            norm_in("b", 0)
            b_main(0)
            experts_out("b", 0)
            with dve.Fori(1, NSEQ) as i:
                norm_in("a", i)
                a_main(i)
                norm_in("c", i - 1)
                a_out(i)
                c_main(i - 1)
                norm_in("b", i)
                c_out(i - 1)
                b_main(i)
                norm_in("d", i - 1)
                experts_out("b", i)
                experts("d", i - 1)
                experts_out("d", i - 1)
            norm_in("c", NSEQ - 1)
            c_main(NSEQ - 1)
            c_out(NSEQ - 1)
            norm_in("d", NSEQ - 1)
            experts("d", NSEQ - 1)
            experts_out("d", NSEQ - 1)


def kernel(**inputs):
    import numpy as np
    import concourse.bacc as bacc
    from concourse.bass_utils import run_bass_kernel_spmd

    v = {k: np.asarray(a) for k, a in inputs.items()}

    def blocks(w):
        return w.reshape(-1, P, w.shape[-1]).transpose(1, 0, 2)

    wq = v["L0_attn_Wq"].reshape(C, NG, 4, HALF, 2)
    wk = v["L0_attn_Wk"].reshape(C, KV0, HALF, 2)
    w1 = np.concatenate([v["L0_ffn_spec_w1"], v["L0_ffn_shared_w1"][None]])
    b1 = np.concatenate([v["L0_ffn_spec_b1"], v["L0_ffn_shared_b1"][None]])
    w2 = np.concatenate([v["L0_ffn_spec_w2"], v["L0_ffn_shared_w2"][None]])
    b2 = np.concatenate([v["L0_ffn_spec_b2"], v["L0_ffn_shared_b2"][None]])
    f32 = np.float32
    inv_freq = f32(1.0) / f32(10000.0) ** (np.arange(0, D0, 2, dtype=f32) / f32(D0))
    angle = (np.arange(T, dtype=f32)[None, :] * inv_freq[:, None]).astype(f32)
    bf16 = mybir.dt.np(BF16)
    arrays = {
        "x": v["L0_attn_x"].reshape(NSEQ, NB, P, C).transpose(0, 2, 1, 3),
        "wqa": wq[..., 0].reshape(C, NG, P), "wqb": wq[..., 1].reshape(C, NG, P),
        "wka": wk[..., 0].reshape(C, P), "wkb": wk[..., 1].reshape(C, P),
        "wv0": v["L0_attn_Wv"], "wo": blocks(v["L0_attn_Wo"]),
        "cos": np.tile(np.cos(angle), (4, 1)), "sin": np.tile(np.sin(angle), (4, 1)),
        "ident": np.eye(P, dtype=f32), "identb": np.eye(P, dtype=f32).astype(bf16),
        "maskb": np.triu(np.full((P, P), -BIG, f32), 1).astype(bf16),
        "f0w1": w1.transpose(2, 0, 1), "f0b1": b1.reshape(E0 + 1, NF, P).transpose(2, 0, 1),
        "f0w2": w2.transpose(2, 0, 1).reshape(NF, P, E0 + 1, C).transpose(1, 2, 0, 3), "f0b2": b2,
        "r0w": v["L0_ffn_router_w"].T, "r0b": np.broadcast_to(v["L0_ffn_router_b"], (P, E0)),
        "w1q": v["L1_attn_w_Q"], "w1k": v["L1_attn_w_K"], "w1v": v["L1_attn_w_V"],
        "f1w1": v["L1_ffn_We1"].transpose(1, 0, 2), "f1b1": v["L1_ffn_be1"].reshape(E1, NF, P).transpose(2, 0, 1),
        "f1w2": v["L1_ffn_We2"].reshape(E1, NF, P, C).transpose(2, 0, 1, 3), "f1b2": v["L1_ffn_be2"],
        "r1w1": v["L1_ffn_rW1"], "r1b1": v["L1_ffn_rb1"].reshape(2, P).T,
        "r1w2": blocks(v["L1_ffn_rW2"]), "r1b2": np.broadcast_to(v["L1_ffn_rb2"], (P, E1)),
    }
    nc = bacc.Bacc("TRN2", target_bir_lowering=False, num_devices=1)
    arrays = {k: np.ascontiguousarray(a) for k, a in arrays.items()}
    io = {k: nc.dram_tensor(k, a.shape, mybir.dt.from_np(a.dtype), kind="ExternalInput").ap()
          for k, a in arrays.items()}
    io["out"] = nc.dram_tensor("out", (NSEQ, P, NB, C), F32, kind="ExternalOutput").ap()
    sandwich_kernel(nc, io)
    r = run_bass_kernel_spmd(nc, [arrays], core_ids=[0])
    return r.results[0]["out"].transpose(0, 2, 1, 3).reshape(NSEQ, T, C)
```

```python
from contextlib import ExitStack

import concourse.bass as bass
from concourse import mybir
from concourse.alu_op_type import AluOpType as ALU

ACT = mybir.ActivationFunctionType
F32 = mybir.dt.float32
F32R = mybir.dt.float32r
BF16 = mybir.dt.bfloat16
AX_X = mybir.AxisListType.X

P = 128
NSEQ, T, C = 8, 512, 128
NB = T // P
H0, KV0, D0 = 16, 4, 64
HALF = D0 // 2
NG = H0 // 4
H1, D1 = 16, 8
E0, E1 = 8, 4
FF = 512
NF = FF // P
EPS = 1e-5
BIG = 1e30
UNITS = H0 * NB
SEG = [P * (i * (i + 1) // 2) for i in range(NB)]
HEADW = P * NB * (NB + 1) // 2
TSEG = [0, 512, 1024, 896]
TBANK = [(4, 0), (5, 0), (6, 0), (5, 384)]
ROWS1 = 9 * D1
MROW = 96
SC1 = float(D1) ** -0.5
KSTACK_DMAS, QSTACK_DMAS = 8, 4
RING = 3
YBANK, SBANK = 7, 3


def expert_pieces(n):
    order = [("up", e, f) for e in range(2) for f in range(NF)] + [("bias", 0, 0)]
    for e in range(n):
        order += [("down", e, t) for t in range(NB)]
        if e + 2 < n:
            order += [("up", e + 2, f) for f in range(NF)]
    return order


def interleave(n, experts):
    pieces = expert_pieces(n) if experts else []
    head = pieces[:NF * 2 + 1 + 12]
    tail = pieces[len(pieces) - 8:] if experts else []
    body = pieces[len(head):len(pieces) - len(tail)]
    order, used = list(head) + [("stack", 0, 0)], 0
    for u in range(4 * H1):
        order.append(("max", u, 0))
        while used < len(body) * (u + 1) // (4 * H1):
            order.append(body[used])
            used += 1
    return order + tail[:4] + [("turn", 0, 0)] + tail[4:]


def sandwich_kernel(nc, io):
    with ExitStack() as ctx:
        base = (nc.sbuf_base + 63) // 64 * 64
        top = [base]

        def size(shape, dt):
            n = 2 if dt == BF16 else 4
            for s in shape[1:]:
                n *= s
            return (n + 31) // 32 * 32

        def sb(name, shape, dt=F32):
            t = nc.alloc_sbuf_tensor_at(name, shape, dt, offset=top[0])
            top[0] += size(shape, dt)
            return t

        def region(kib):
            at = top[0]
            top[0] += kib * 1024
            return [at, at + kib * 1024]

        def sub(reg, name, shape, dt=F32):
            t = nc.alloc_sbuf_tensor_at(name, shape, dt, offset=reg[0])
            reg[0] += size(shape, dt)
            assert reg[0] <= reg[1], name
            return t

        def sem(name):
            return ctx.enter_context(nc.semaphore(name))

        ps = ctx.enter_context(nc.psum_tensor("ps", [P, 8, 512], F32))

        wqa, wqb = sb("wqa", [P, NG, P]), sb("wqb", [P, NG, P])
        wka, wkb = sb("wka", [P, P]), sb("wkb", [P, P])
        wv0 = sb("wv0", [P, KV0 * D0])
        wo = sb("wo", [P, H0 * D0 // P, C])
        cos, sin = sb("cos", [P, T]), sb("sin", [P, T])
        ident, identb, maskb = sb("ident", [P, P]), sb("identb", [P, P], BF16), sb("maskb", [P, P], BF16)
        f0w1, f0b1 = sb("f0w1", [P, E0 + 1, FF]), sb("f0b1", [P, E0 + 1, NF])
        f0w2, f0b2 = sb("f0w2", [P, E0 + 1, NF, C]), sb("f0b2", [E0 + 1, C])
        r0w, r0b = sb("r0w", [P, E0]), sb("r0b", [P, E0])
        w1q, w1k, w1v = sb("w1q", [P, P]), sb("w1k", [P, P]), sb("w1v", [P, P])
        f1w1, f1b1 = sb("f1w1", [P, E1, FF]), sb("f1b1", [P, E1, NF])
        f1w2, f1b2 = sb("f1w2", [P, E1, NF, C]), sb("f1b2", [E1, C])
        r1w1, r1b1 = sb("r1w1", [P, 2 * P]), sb("r1b1", [P, 2])
        r1w2, r1b2 = sb("r1w2", [P, 2, E1]), sb("r1b2", [P, E1])
        ranks = sb("ranks", [P, E0])
        neghalf = sb("neghalf", [P, NB])
        x0, x1, x2, x3 = (sb(f"x{i}", [P, NB, C]) for i in range(4))
        xn = sb("xn", [P, NB, C])
        xta, xtb = sb("xta", [P, T]), sb("xtb", [P, T])
        st, mv, rstd = sb("st", [P, NB, 6]), sb("mv", [P, NB, 2]), sb("rstd", [P, NB])
        acc = sb("acc", [P, NB, C])
        r_q = region(32)
        qs = nc.alloc_sbuf_tensor_at("qs", [P, H0, T], F32R, offset=r_q[0])
        pt1 = sub(r_q, "pt1", [P, 4, 2, T])
        zt = sub(r_q, "zt", [P, 4, T])
        parts = sub(r_q, "parts", [P, 3, 2, T], BF16)
        r_k = region(16)
        ks1 = nc.alloc_sbuf_tensor_at("ks1", [P, KV0, T], F32R, offset=r_k[0])
        ks2 = nc.alloc_sbuf_tensor_at("ks2", [P, KV0, T], F32R, offset=r_k[0] + 8192)
        qd = sub(r_k, "qd", [P, H1, T], BF16)
        r_h = region(16)
        hi = nc.alloc_sbuf_tensor_at("hi", [P, 2, 2, T], F32R, offset=r_h[0])
        lo = nc.alloc_sbuf_tensor_at("lo", [P, 2, 2, T], F32R, offset=r_h[0] + 8192)
        kd = sub(r_h, "kd", [P, H1, T], BF16)
        r_t = region(16)
        hid0 = nc.alloc_sbuf_tensor_at("hid0", [P, NF, T], F32, offset=r_t[0] + 8192)
        yt = nc.alloc_sbuf_tensor_at("yt", [P, H0 // 2, T], F32, offset=r_t[0])
        tmp = nc.alloc_sbuf_tensor_at("tmp", [P, NB, C], F32, offset=r_t[0])
        t12 = sub(r_t, "t12", [P, 2, T])
        t34 = sub(r_t, "t34", [P, 2, T])
        r_p = region(25)
        hid = [hid0,
               nc.alloc_sbuf_tensor_at("hid1", [P, NF, T], F32, offset=r_p[0] + 16384)]
        rh = nc.alloc_sbuf_tensor_at("rh", [P, 2, T], F32, offset=r_p[0] + 16384)
        rab = nc.alloc_sbuf_tensor_at("rab", [P, 2, 2, T], F32, offset=r_p[0])
        oab = nc.alloc_sbuf_tensor_at("oab", [P, 2, 2, T], F32, offset=r_p[0] + 8192)
        pb = sub(r_p, "pb", [P, 2, HEADW])
        ptt = sub(r_p, "ptt", [P, 3, HEADW])
        r_v = region(4)
        v0 = nc.alloc_sbuf_tensor_at("v0", [P, NB, KV0 * D0], F32, offset=r_v[0])
        res = sub(r_v, "res", [P, 2, T])
        vs = sb("vs", [P, NB, H1, 32])
        combt = nc.alloc_sbuf_tensor_at("combt", [E0 + 1, T], F32, offset=top[0])
        mt = nc.alloc_sbuf_tensor_at("mt", [48, T], BF16, offset=top[0])
        top[0] += 4 * T
        nm = sb("nm", [P, 8])
        sums, rsum = sb("sums", [P, 2, NB]), sb("rsum", [P, 2, NB])
        r_s = [top[0], top[0] + 1152]
        rt = {k: nc.alloc_sbuf_tensor_at("rt_" + k, [P, NB, E0 + 1], F32, offset=r_s[0] + 160 * n)
              for n, k in enumerate(("lg", "eq", "oh1", "msk", "ex"))}
        nm1, nm1r = sub(r_s, "nm1", [P, NB, H1]), sub(r_s, "nm1r", [P, NB, H1])
        nmp = sub(r_s, "nmp", [P, NB, 3, H1], BF16)
        rc1 = sub(r_s, "rc1", [P, NB * H1])
        top[0] += 1152
        rt["comb"] = sb("comb", [P, NB, E0 + 1])
        rm = sb("rm", [P, 4, NB])
        assert top[0] <= nc.sbuf_usable_end, (top[0], nc.sbuf_usable_end)

        rotated = nc.dram_tensor("rotated", [1 + NG, 2, P, 2, T], F32).ap()
        scratch = nc.dram_tensor("scratch", [2, 3, P, T], BF16).ap()

        s_w = sem("s_w"); s_comb1 = sem("s_comb1"); s_const = sem("s_const"); s_wscaled = sem("s_wscaled")
        NWA, NWF = 11, 16
        s_wf = sem("s_wf")
        a_in = sem("a_in"); a_krope = sem("a_krope")
        stats = {k: sem("stats_" + k) for k in ("ai", "ao", "bi", "bo", "ci", "co", "di", "do")}
        rs_ready = {k: sem("rs_" + k) for k in ("ai", "ao", "bi", "bo", "ci", "co", "di", "do")}
        xn_ready = {k: sem("xn_" + k) for k in "abcd"}
        xt_ps = {k: sem("xtps_" + k) for k in "abcd"}
        xt_ready = {k: sem("xt_" + k) for k in "abcd"}
        res_done = {k: sem("res_" + k) for k in "abcd"}
        chain = {k: sem("chain_" + k) for k in "abcd"}
        pch = {k: sem("pch_" + k) for k in "abcd"}
        a_pair_ps = sem("a_pair_ps"); a_pair_act = sem("a_pair_act"); a_t12 = sem("a_t12")
        a_oa = sem("a_oa"); a_ob = sem("a_ob"); a_hi = sem("a_hi"); a_lo = sem("a_lo")
        a_v_ps = sem("a_v_ps"); a_v = sem("a_v")
        a_scr = sem("a_scr")
        a_kst = sem("a_kst"); a_qst = [sem(f"a_qst{g}") for g in range(NG)]
        a_s = sem("a_s"); a_nm = sem("a_nm"); a_exp = sem("a_exp")
        a_pn = sem("a_pn"); a_tr = sem("a_tr"); a_pt_act = sem("a_pt_act"); a_pt_dve = sem("a_pt_dve")
        a_y_ps = sem("a_y_ps"); a_yt = sem("a_yt")
        a_o_ps = sem("a_o_ps")
        c_qk_ps = sem("c_qk_ps"); c_v_ps = sem("c_v_ps"); c_v = sem("c_v"); c_parts = sem("c_parts")
        c_scr = sem("c_scr"); c_stack = sem("c_stack"); c_pad = sem("c_pad")
        c_s1 = sem("c_s1"); c_nm = sem("c_nm")
        c_nmp = sem("c_nmp"); c_mt_ps = sem("c_mt_ps"); c_mt = sem("c_mt"); c_mrow = sem("c_mrow")
        c_s2 = sem("c_s2"); c_exp = sem("c_exp")
        c_pv = sem("c_pv"); c_z = sem("c_z")
        c_x3 = sem("c_x3"); c_zt = sem("c_zt"); c_att = sem("c_att")
        f_rps = {k: sem("rps_" + k) for k in "bd"}; f_lm = {k: sem("lm_" + k) for k in "bd"}
        f_ex = {k: sem("ex_" + k) for k in "bd"}; f_comb = {k: sem("comb_" + k) for k in "bd"}
        f_ctps = {k: sem("ctps_" + k) for k in "bd"}; f_ct = {k: sem("ct_" + k) for k in "bd"}
        f_bias_ps = {k: sem("biasps_" + k) for k in "bd"}; f_bias = {k: sem("bias_" + k) for k in "bd"}
        f_h = {k: sem("h_" + k) for k in "bd"}; f_g = {k: sem("g_" + k) for k in "bd"}
        f_y = {k: sem("y_" + k) for k in "bd"}; f_acc = {k: sem("acc_" + k) for k in "bd"}
        d_rh_ps = sem("d_rh_ps"); d_rh = sem("d_rh")
        pool_dma = sem("pool_dma")

        XT = {"a": xta, "c": xtb, "b": xta, "d": xtb}
        XTBANK = SBANK
        SRC = {"a": x0, "b": x1, "c": x2, "d": x3}
        DST = {"a": x1, "b": x2, "c": x3, "d": x3}
        FFN = {"b": dict(n=E0 + 1, routed=E0, w1=f0w1, b1=f0b1, w2=f0w2, b2=f0b2, rb=r0b),
               "d": dict(n=E1, routed=E1, w1=f1w1, b1=f1b1, w2=f1w2, b2=f1b2, rb=r1b2)}

        x_dram, out_dram = io["x"], io["out"]
        block = ctx.enter_context(nc.Block())


        @block.sync
        def _(sp):
            for n, (name, dst) in enumerate((("wka", wka), ("wkb", wkb), ("wv0", wv0), ("cos", cos), ("sin", sin),
                              ("ident", ident), ("identb", identb), ("maskb", maskb), ("wqa", wqa), ("wqb", wqb),
                              ("wo", wo), ("r0w", r0w), ("r0b", r0b), ("f0b1", f0b1), ("f0b2", f0b2),
                              ("f0w1", f0w1), ("f0w2", f0w2), ("w1q", w1q), ("w1k", w1k), ("w1v", w1v),
                              ("r1w1", r1w1), ("r1b1", r1b1), ("r1w2", r1w2),
                              ("f1b1", f1b1), ("f1b2", f1b2), ("f1w1", f1w1), ("f1w2", f1w2))):
                if n == 0:
                    sp.dma_start(x0[:], x_dram[0]).then_inc(a_in, 16)
                sp.dma_start(dst[:], io[name]).then_inc(s_w if n < NWA else s_wf, 16)

            def a_rope(b):
                if not (isinstance(b, int) and b == 0):
                    sp.wait_ge(res_done["a"], b)
                    sp.dma_start(x0[:], x_dram[b]).then_inc(a_in, 16)
                for p in range(1 + NG):
                    sp.wait_ge(a_hi, 5 * b + p + 1)
                    sp.dma_start(rotated[p, 0], hi[:, p % 2].bitcast(F32)).then_inc(a_scr, 16)
                    sp.wait_ge(a_lo, 5 * b + p + 1)
                    sp.dma_start(rotated[p, 1], lo[:, p % 2].bitcast(F32)).then_inc(a_scr, 16)
                    sp.wait_ge(a_scr, 160 * b + 32 * p + 32)
                    for r in range(4):
                        src = rotated[p, r // 2, :, r % 2, :].rearrange("(h j) t -> j h t", j=HALF)
                        rows = slice(HALF * r, HALF * r + HALF)
                        if p == 0:
                            swapped = slice(HALF * ((r + 2) % 4), HALF * ((r + 2) % 4) + HALF)
                            sp.dma_start(ks1[rows, :, :].bitcast(F32), src).then_inc(a_kst, 16)
                            sp.dma_start(ks2[swapped, :, :].bitcast(F32), src).then_inc(a_kst, 16)
                        else:
                            sp.dma_start(qs[rows, 4 * (p - 1):4 * p, :].bitcast(F32), src).then_inc(a_qst[p - 1], 16)

            def c_main(b):
                sp.wait_ge(c_parts, b + 1)
                for w in range(2):
                    sp.dma_start(scratch[w].rearrange("s p t -> p s t"), parts[:, :, w, :]).then_inc(c_scr, 16)
                sp.wait_ge(c_scr, 32 * b + 32)
                sp.wait_ge(c_pad, 3 * b + 3)
                for s in range(3):
                    for s2 in range(3):
                        r = (3 * s + s2) * D1
                        sp.dma_start(qd[r:r + D1, :, :],
                                     scratch[0, s].rearrange("(h d) t -> d h t", d=D1)).then_inc(c_stack, 16)
                        sp.dma_start(kd[r:r + D1, :, :],
                                     scratch[1, s2].rearrange("(h d) t -> d h t", d=D1)).then_inc(c_stack, 16)
                sp.wait_ge(c_mt, b + 1)
                for s in range(3):
                    sp.dma_start(qd[MROW + s:MROW + s + 1, :, :], mt[16 * s:16 * s + 16, :]).then_inc(c_mrow, 16)

            a_rope(0)
            a_rope(1)
            with sp.Fori(1, NSEQ - 1) as i:
                c_main(i - 1)
                a_rope(i + 1)
            c_main(NSEQ - 2)
            c_main(NSEQ - 1)

        @block.gpsimd
        def _(pool):
            pool.memset(neghalf[:], -0.5).then_inc(s_const, 1)
            pool.memset(vs[:], 0.0).then_inc(s_const, 1)
            pool.dma_start(r1b2[:], io["r1b2"]).then_inc(pool_dma, 16)
            pool.wait_ge(s_const, 2)
            pool.memset(vs[:, :, :, D1:D1 + 1], 1.0).then_inc(s_const, 1)
            for e in range(E0):
                pool.memset(ranks[:, e:e + 1], float(E0 - e)).then_inc(s_const, 1)
            pool.wait_ge(s_const, 3 + E0)

            def norm_scale(k, which, b, n):
                pool.wait_ge(stats[which], b + 1)
                pool.nop(nofuse=True)
                pool.tensor_scalar(rstd[:], mv[:, :, 1], EPS, None, ALU.add).then_inc(pch[k], 1)
                pool.wait_ge(pch[k], PCH[k] * b + n)
                pool.tensor_tensor(rstd[:], rstd[:], neghalf[:], ALU.pow).then_inc(rs_ready[which], 1)

            PCH = {"a": 2 + 5, "b": 2, "c": 2, "d": 2}

            def a_rope(b, start, end):
                for p in range(start, end):
                    pool.wait_ge(a_pair_act, 5 * b + p + 1)
                    if p > 0:
                        pool.wait_ge(a_ob, 5 * b + p)
                    pool.tensor_tensor(t34[:, 0, :], rab[:, p % 2, 0, :], sin[:], ALU.mult)
                    pool.tensor_tensor(t34[:, 1, :], rab[:, p % 2, 1, :], cos[:], ALU.mult).then_inc(pch["a"], 1)
                    pool.wait_ge(pch["a"], PCH["a"] * b + 1 + p + 1)
                    if p > 1:
                        pool.wait_ge(a_hi, 5 * b + p - 1)
                        pool.wait_ge(a_lo, 5 * b + p - 1)
                    pool.tensor_tensor(oab[:, p % 2, 1, :], t34[:, 0, :], t34[:, 1, :], ALU.add).then_inc(a_ob, 1)

            def c_in(b):
                norm_scale("c", "ci", b, 1)
                pool.wait_ge(xt_ready["c"], b + 1)
                pool.nop(nofuse=True)
                pool.memset(qd[64:P, :, :].bitcast(F32), 0.0).then_inc(c_pad, 1)
                pool.wait_ge(c_pad, 3 * b + 1)
                pool.nop(nofuse=True)
                pool.memset(kd[64:MROW, :, :].bitcast(F32), 0.0).then_inc(c_pad, 1)
                pool.wait_ge(c_pad, 3 * b + 2)
                pool.nop(nofuse=True)
                pool.memset(kd[MROW:P, :, :], 1.0).then_inc(c_pad, 1)
                pool.wait_ge(c_pad, 3 * b + 3)
                pool.nop(nofuse=True)

            def d_out(b):
                norm_scale("d", "do", b, 2)
                pool.wait_ge(res_done["d"], b + 1)
                pool.dma_start(out_dram[b], x3[:]).then_inc(pool_dma, 16)

            def phase_a(a, d):
                a_rope(a, 0, 2)
                if d is not None:
                    norm_scale("d", "di", d, 1)
                a_rope(a, 2, 1 + NG)
                if d is not None:
                    d_out(d)

            pool.wait_ge(s_w, 16 * NWA)
            norm_scale("a", "ai", 0, 1)
            phase_a(0, None)
            norm_scale("a", "ao", 0, 2 + 5)
            norm_scale("b", "bi", 0, 1)
            norm_scale("b", "bo", 0, 2)
            norm_scale("a", "ai", 1, 1)
            phase_a(1, None)
            with pool.Fori(1, NSEQ - 1) as i:
                c_in(i - 1)
                norm_scale("a", "ao", i, 2 + 5)
                norm_scale("b", "bi", i, 1)
                norm_scale("b", "bo", i, 2)
                norm_scale("a", "ai", i + 1, 1)
                norm_scale("c", "co", i - 1, 2)
                phase_a(i + 1, i - 1)
            for n in (NSEQ - 2, NSEQ - 1):
                c_in(n)
                if n == NSEQ - 2:
                    norm_scale("a", "ao", NSEQ - 1, 2 + 5)
                    norm_scale("b", "bi", NSEQ - 1, 1)
                    norm_scale("b", "bo", NSEQ - 1, 2)
                norm_scale("c", "co", n, 2)
                norm_scale("d", "di", n, 1)
                d_out(n)
            pool.wait_ge(pool_dma, 16 * (NSEQ + 1))

        @block.tensor
        def _(pe):
            def to_channels(k, b):
                pe.wait_ge(xn_ready[k], b + 1)
                for t in range(NB):
                    last = pe.transpose(ps[:, XTBANK, t * P:t * P + P], xn[:, t, :], ident[:])
                last.then_inc(xt_ps[k], 1)

            def a_pair(b, p):
                if p == 0:
                    pe.wait_ge(xt_ready["a"], b + 1)
                else:
                    pe.wait_ge(a_pair_act, 5 * b + p)
                if p == 1 and isinstance(b, int):
                    pe.wait_ge(s_wscaled, 2)
                pe.matmul(ps[:, 0, :], wka[:] if p == 0 else wqa[:, p - 1, :], xta[:], start=True, stop=True)
                pe.matmul(ps[:, 1, :], wkb[:] if p == 0 else wqb[:, p - 1, :], xta[:], start=True,
                          stop=True).then_inc(a_pair_ps, 1)
                if p < 2:
                    if p == 1:
                        pe.wait_ge(a_v, 2 * b + 1)
                    for t in range(2 * p, 2 * p + 2):
                        last = pe.matmul(ps[:, 2, 256 * (t % 2):256 * (t % 2) + 256],
                                         xta[:, t * P:t * P + P], wv0[:], start=True, stop=True)
                    last.then_inc(a_v_ps, 1)

            def a_main(b):
                pe.wait_ge(a_pair_act, 5 * b + 5)
                pe.wait_ge(a_v, 2 * b + 2)
                pe.wait_ge(a_kst, 16 * KSTACK_DMAS * b + 16 * KSTACK_DMAS)

                def scores(h):
                    if h % 4 == 0:
                        pe.wait_ge(a_qst[h // 4], 16 * QSTACK_DMAS * b + 16 * QSTACK_DMAS)
                    for i in range(NB):
                        u = NB * h + i
                        n = P * (i + 1)
                        if u >= 4:
                            pe.wait_ge(a_exp, UNITS * b + u - 3)
                        q = qs[:, h, P * i:P * i + P]
                        s = ps[:, u % 4, 0:n]
                        pe.matmul(ps[:, u % 4, n - P:n], identb[:], maskb[:], start=True, stop=False,
                                  skip_group_check=True)
                        pe.matmul(s, q, ks1[:, h // 4, 0:n], start=False, stop=False, skip_group_check=True)
                        pe.matmul(s, q, ks2[:, h // 4, 0:n], start=False, stop=True,
                                  skip_group_check=True).then_inc(a_s, 1)

                def transposes(h):
                    pe.wait_ge(a_pn, H0 * b + h + 1)
                    if h > 0:
                        pe.wait_ge(a_pt_act, H0 * b + h)
                        pe.wait_ge(a_pt_dve, H0 * b + h)
                    for i in range(NB):
                        for kb in range(i + 1):
                            bank, col = TBANK[kb]
                            col += P * (i - kb)
                            last = pe.transpose(ps[:, bank, col:col + P],
                                                pb[:, h % 2, SEG[i] + P * kb:SEG[i] + P * kb + P], ident[:])
                    last.then_inc(a_tr, 1)

                def weighted_values(j):
                    pe.wait_ge(a_pt_act, H0 * b + 2 * j + 2)
                    pe.wait_ge(a_pt_dve, H0 * b + 2 * j + 2)
                    if j > 0:
                        pe.wait_ge(a_yt, (H0 // 2) * b + j)
                    kv = j // 2
                    for kb in range(NB):
                        for s in range(2):
                            n = T - P * kb
                            last = pe.matmul(ps[64 * s:64 * s + 64, 7, P * kb:T],
                                             v0[:, kb, D0 * kv:D0 * kv + D0],
                                             ptt[:, (2 * j + s) % 3, TSEG[kb]:TSEG[kb] + n],
                                             start=(kb == 0), stop=(kb == NB - 1), skip_group_check=True)
                    last.then_inc(a_y_ps, 1)

                for s in range(H0 + 2):
                    if s < H0:
                        scores(s)
                    if 1 <= s <= H0:
                        transposes(s - 1)
                    if s >= 3 and s % 2:
                        weighted_values((s - 3) // 2)

            def a_out(b):
                pe.wait_ge(a_yt, (H0 // 2) * b + H0 // 2)
                for t in range(NB):
                    for j in range(H0 // 2):
                        last = pe.matmul(ps[:, 7, t * P:t * P + P], yt[:, j, t * P:t * P + P], wo[:, j, :],
                                         start=(j == 0), stop=(j == H0 // 2 - 1))
                last.then_inc(a_o_ps, 1)

            def c_project(b):
                pe.wait_ge(xt_ready["c"], b + 1)
                pe.matmul(ps[:, 0, :], w1q[:], xtb[:], start=True, stop=True)
                pe.matmul(ps[:, 1, :], w1k[:], xtb[:], start=True, stop=True).then_inc(c_qk_ps, 1)
                for t in range(NB):
                    last = pe.matmul(ps[:, 2, t * P:t * P + P], xtb[:, t * P:t * P + P], w1v[:],
                                     start=True, stop=True)
                last.then_inc(c_v_ps, 1)

            def c_max_scores(b, u):
                i, h = u // H1, u % H1
                if u >= 3:
                    pe.wait_ge(c_nm, 64 * b + u - 2)
                pe.matmul(ps[:, u % 3, :], qd[:, h, i * P:i * P + P], kd[:, h, :], start=True,
                          stop=True).then_inc(c_s1, 1)

            def c_turn(b):
                pe.wait_ge(c_nmp, b + 1)
                pe.nop(nofuse=True)
                mtp = ps[0:48, SBANK, 0:T // 2].bitcast(BF16)
                for t in range(NB):
                    last = pe.transpose(mtp[:, t * P:t * P + P],
                                        nmp[:, t, :, :].rearrange("p s h -> p (s h)"), identb[:])
                last.then_inc(c_mt_ps, 1)

            def c_main(b):
                pe.wait_ge(c_mrow, 48 * b + 48)

                def scores(w):
                    hg, kb, gp = w // 8, (w // 2) % 4, w % 2
                    if w >= 3:
                        pe.wait_ge(c_exp, 32 * b + w - 2)
                    for g in range(2):
                        h = 4 * hg + 2 * gp + g
                        last = pe.matmul(ps[:, 2 * (w % 3) + g, :], kd[:, h, kb * P:kb * P + P], qd[:, h, :],
                                         start=True, stop=True)
                    last.then_inc(c_s2, 1)

                def weighted_values(y):
                    hg, kb = y // 4, y % 4
                    pe.wait_ge(c_exp, 32 * b + 2 * y + 2)
                    if kb == 0 and hg >= 2:
                        pe.wait_ge(c_z, 4 * b + hg - 1)
                    for g in range(4):
                        last = pe.matmul(ps[32 * g:32 * g + 32, 6 + hg % 2, :], vs[:, kb, 4 * hg + g, :],
                                         pt1[:, (2 * y + g // 2) % 4, g % 2, :],
                                         start=(kb == 0), stop=(kb == NB - 1), skip_group_check=True)
                    last.then_inc(c_pv, 1)

                for y in range(16 + 1):
                    if y < 16:
                        scores(2 * y)
                        scores(2 * y + 1)
                    if y >= 1:
                        weighted_values(y - 1)

            def c_out(b):
                pe.wait_ge(c_z, 4 * b + 4)
                for i in range(NB):
                    for hg in range(4):
                        last = pe.transpose(ps[:, 4 + i, hg * P:hg * P + P], zt[:, hg, i * P:i * P + P], ident[:])
                last.then_inc(c_zt, 1)

            def piece(k, b, what, e, m):
                g = FFN[k]
                n = g["n"]
                if what == "up":
                    u = NF * e + m
                    if u >= RING:
                        pe.wait_ge(f_g[k], NF * n * b + u - RING + 1)
                    pe.matmul(ps[:, 4 + u % RING, :], g["w1"][:, e, m * P:m * P + P], XT[k][:],
                              start=True, stop=True).then_inc(f_h[k], 1)
                if what == "down":
                    if m == 0:
                        pe.wait_ge(f_g[k], NF * n * b + NF * e + NF)
                        if e >= 1:
                            pe.wait_ge(f_acc[k], n * b + e)
                    for f in range(NF):
                        last = pe.matmul(ps[:, YBANK, m * P:m * P + P], hid[e % 2][:, f, m * P:m * P + P],
                                         g["w2"][:, e, f, :], start=(f == 0), stop=(f == NF - 1))
                    if m == NB - 1:
                        last.then_inc(f_y[k], 1)
                if what == "bias":
                    pe.wait_ge(f_comb[k], b + 1)
                    for t in range(NB):
                        last = pe.transpose(ps[0:n, SBANK, t * P:t * P + P], rt["comb"][:, t, 0:n], ident[:])
                    last.then_inc(f_ctps[k], 1)
                    pe.wait_ge(f_ct[k], b + 1)
                    for t in range(NB):
                        last = pe.matmul(ps[:, SBANK, t * P:t * P + P], combt[0:n, t * P:t * P + P],
                                         g["b2"][0:n, :], start=True, stop=True)
                    last.then_inc(f_bias_ps[k], 1)

            def b_router(b):
                pe.wait_ge(xt_ready["b"], b + 1)
                for t in range(NB):
                    last = pe.matmul(ps[:, SBANK, t * E0:t * E0 + E0], xta[:, t * P:t * P + P], r0w[:],
                                     start=True, stop=True)
                last.then_inc(f_rps["b"], 1)

            def d_router(b):
                pe.wait_ge(xt_ready["d"], b + 1)
                for f in range(2):
                    pe.matmul(ps[:, 4 + f, :], r1w1[:, f * P:f * P + P], xtb[:], start=True,
                              stop=True).then_inc(d_rh_ps, 1)

            def d_logits(b):
                pe.wait_ge(d_rh, 2 * b + 2)
                for t in range(NB):
                    for f in range(2):
                        last = pe.matmul(ps[:, SBANK, t * E1:t * E1 + E1], rh[:, f, t * P:t * P + P],
                                         r1w2[:, f, :], start=(f == 0), stop=(f == 1))
                last.then_inc(f_rps["d"], 1)

            def phase_a(a, d):
                a_pair(a, 0)
                a_pair(a, 1)
                if d is not None:
                    to_channels("d", d)
                a_pair(a, 2)
                if d is not None:
                    d_router(d)
                a_pair(a, 3)
                if d is not None:
                    d_logits(d)
                a_pair(a, 4)
                if d is not None:
                    for what, e, m in expert_pieces(E1):
                        piece("d", d, what, e, m)
                a_main(a)

            def phase_b(b, c):
                c_project(c)
                if b is not None:
                    to_channels("b", b)
                    b_router(b)
                for what, e, m in interleave(E0 + 1, b is not None):
                    if what == "stack":
                        pe.wait_ge(c_v, c + 1)
                        pe.wait_ge(c_stack, 16 * 18 * c + 16 * 18)
                    elif what == "max":
                        c_max_scores(c, e)
                    elif what == "turn":
                        c_turn(c)
                    else:
                        piece("b", b, what, e, m)
                if b is not None:
                    pe.wait_ge(f_acc["b"], (E0 + 1) * b + E0 + 1)
                c_main(c)

            pe.wait_ge(s_w, 16 * NWA)
            to_channels("a", 0)
            phase_a(0, None)
            a_out(0)
            to_channels("b", 0)
            pe.wait_ge(s_wf, 16 * NWF)
            b_router(0)
            for what, e, m in expert_pieces(E0 + 1):
                piece("b", 0, what, e, m)
            to_channels("a", 1)
            phase_a(1, None)
            with pe.Fori(1, NSEQ - 1) as i:
                to_channels("c", i - 1)
                a_out(i)
                phase_b(i, i - 1)
                to_channels("a", i + 1)
                c_out(i - 1)
                phase_a(i + 1, i - 1)
            to_channels("c", NSEQ - 2)
            a_out(NSEQ - 1)
            phase_b(NSEQ - 1, NSEQ - 2)
            for n in (NSEQ - 2, NSEQ - 1):
                c_out(n)
                to_channels("d", n)
                d_router(n)
                d_logits(n)
                for what, e, m in expert_pieces(E1):
                    piece("d", n, what, e, m)
                if n == NSEQ - 2:
                    to_channels("c", n + 1)
                    phase_b(None, n + 1)

        @block.scalar
        def _(act):
            act.wait_ge(s_w, 16 * NWA)
            act.activation(wqa[:], wqa[:], ACT.Copy, scale=float(D0) ** -0.5).then_inc(s_wscaled, 1)
            act.activation(wqb[:], wqb[:], ACT.Copy, scale=float(D0) ** -0.5).then_inc(s_wscaled, 1)

            def copy_channels(k, b):
                act.wait_ge(xt_ps[k], b + 1)
                act.activation(XT[k][:], ps[:, XTBANK, :], ACT.Copy).then_inc(xt_ready[k], 1)

            def a_take(b, p):
                act.wait_ge(a_pair_ps, 5 * b + p + 1)
                if p >= 2:
                    act.wait_ge(a_ob, 5 * b + p - 1)
                    act.wait_ge(a_oa, 5 * b + p - 1)
                act.activation(rab[:, p % 2], ps[:, 0:2, :], ACT.Copy).then_inc(a_pair_act, 1)
                if p < 2:
                    act.wait_ge(a_v_ps, 2 * b + p + 1)
                    act.activation(v0[:, 2 * p:2 * p + 2, :].rearrange("p t c -> p (t c)"), ps[:, 2, :],
                                   ACT.Copy).then_inc(a_v, 1)

            def a_high(b, p):
                act.wait_ge(a_oa, 5 * b + p + 1)
                act.wait_ge(a_ob, 5 * b + p + 1)
                if p >= 2:
                    act.wait_ge(a_scr, 160 * b + 32 * (p - 1))
                act.activation(hi[:, p % 2], oab[:, p % 2], ACT.Copy).then_inc(a_hi, 1)

            def a_main(b):
                def softmax(h):
                    for i in range(NB):
                        u = NB * h + i
                        n = P * (i + 1)
                        act.wait_ge(a_nm, UNITS * b + u + 1)
                        if i == 0 and h >= 2:
                            act.wait_ge(a_tr, H0 * b + h - 1)
                        act.activation(pb[:, h % 2, SEG[i]:SEG[i] + n], ps[:, u % 4, 0:n], ACT.Exp,
                                       bias=nm[:, u % 8:u % 8 + 1],
                                       accum_out=sums[:, h % 2, i:i + 1]).then_inc(a_exp, 1)

                for s in range(H0 + 2):
                    if s < H0:
                        softmax(s)
                    if 1 <= s <= H0:
                        h = s - 1
                        act.wait_ge(a_tr, H0 * b + h + 1)
                        if h >= 3:
                            act.wait_ge(a_y_ps, (H0 // 2) * b + (h - 3) // 2 + 1)
                        act.activation(ptt[:, h % 3, 512:HEADW],
                                       ps[:, 5:7, :].rearrange("p a c -> p (a c)")[:, 0:768],
                                       ACT.Copy).then_inc(a_pt_act, 1)
                    if s >= 3 and s % 2:
                        j = (s - 3) // 2
                        act.wait_ge(a_y_ps, (H0 // 2) * b + j + 1)
                        act.activation(yt[:, j, :], ps[:, 7, :], ACT.Copy).then_inc(a_yt, 1)

            def c_values(b):
                act.wait_ge(c_v_ps, b + 1)
                act.activation(vs[:, :, :, 0:D1].rearrange("p t h d -> p (t h) d"),
                               ps[:, 2, :].rearrange("p (t d) -> p t d", d=D1), ACT.Copy).then_inc(c_v, 1)

            def c_main(b):
                for w in range(32):
                    act.wait_ge(c_s2, 32 * b + w + 1)
                    if w >= 4:
                        act.wait_ge(c_pv, 16 * b + (w - 4) // 2 + 1)
                    bank = 2 * (w % 3)
                    act.activation(pt1[:, w % 4], ps[:, bank:bank + 2, :], ACT.Exp, scale=SC1).then_inc(c_exp, 1)

            def routing(k, b):
                r = FFN[k]["routed"]
                act.wait_ge(f_lm[k], b + 1)
                act.activation(rt["ex"][:, :, 0:r], rt["lg"][:, :, 0:r], ACT.Exp).then_inc(f_ex[k], 1)

            def piece(k, b, what, e, m):
                g = FFN[k]
                n = g["n"]
                if what == "up":
                    u = NF * e + m
                    act.wait_ge(f_h[k], NF * n * b + u + 1)
                    if m == 0 and e >= 2:
                        act.wait_ge(f_y[k], n * b + e - 1)
                    act.activation(hid[e % 2][:, m, :], ps[:, 4 + u % RING, :],
                                   ACT.Gelu_apprx_tanh if k == "b" else ACT.Gelu,
                                   bias=g["b1"][:, e, m:m + 1]).then_inc(f_g[k], 1)
                if what == "bias":
                    act.wait_ge(f_ctps[k], b + 1)
                    act.activation(combt[0:n, :], ps[0:n, SBANK, :], ACT.Copy).then_inc(f_ct[k], 1)

            def d_router(b):
                for f in range(2):
                    act.wait_ge(d_rh_ps, 2 * b + f + 1)
                    act.activation(rh[:, f, :], ps[:, 4 + f, :], ACT.Gelu, bias=r1b1[:, f:f + 1]).then_inc(d_rh, 1)

            def phase_a(a, d):
                a_take(a, 0)
                a_take(a, 1)
                a_high(a, 0)
                if d is not None:
                    copy_channels("d", d)
                a_take(a, 2)
                a_high(a, 1)
                if d is not None:
                    d_router(d)
                a_take(a, 3)
                a_high(a, 2)
                a_take(a, 4)
                a_high(a, 3)
                if d is not None:
                    routing("d", d)
                a_high(a, 4)
                if d is not None:
                    for what, e, m in expert_pieces(E1):
                        piece("d", d, what, e, m)
                a_main(a)

            def phase_b(b, c):
                c_values(c)
                if b is not None:
                    copy_channels("b", b)
                    routing("b", b)
                for what, e, m in interleave(E0 + 1, b is not None):
                    if what == "turn":
                        act.wait_ge(c_mt_ps, c + 1)
                        act.activation(mt[:], ps[0:48, SBANK, 0:T // 2].bitcast(BF16), ACT.Copy).then_inc(c_mt, 1)
                    elif what in ("up", "bias"):
                        piece("b", b, what, e, m)
                c_main(c)

            copy_channels("a", 0)
            phase_a(0, None)
            copy_channels("b", 0)
            act.wait_ge(s_wf, 16 * NWF)
            routing("b", 0)
            for what, e, m in expert_pieces(E0 + 1):
                piece("b", 0, what, e, m)
            copy_channels("a", 1)
            phase_a(1, None)
            with act.Fori(1, NSEQ - 1) as i:
                copy_channels("c", i - 1)
                phase_b(i, i - 1)
                copy_channels("a", i + 1)
                phase_a(i + 1, i - 1)
            copy_channels("c", NSEQ - 2)
            phase_b(NSEQ - 1, NSEQ - 2)
            for n in (NSEQ - 2, NSEQ - 1):
                copy_channels("d", n)
                d_router(n)
                routing("d", n)
                for what, e, m in expert_pieces(E1):
                    piece("d", n, what, e, m)
                if n == NSEQ - 2:
                    copy_channels("c", n + 1)
                    phase_b(None, n + 1)

        @block.vector
        def _(dve):
            CH = {"a": 1 + H0 + 2, "b": 1 + 15 + 2, "c": 1 + 6 + 1 + 2, "d": 1 + 15 + 2}
            done = {}

            def link(k, b, ins):
                done[k] += 1
                ins.then_inc(chain[k], 1)
                dve.wait_ge(chain[k], CH[k] * b + done[k])

            def norm_stats(k, which, b, src):
                for t in range(NB):
                    last = dve.bn_stats(st[:, t, :], src(t))
                link(k, b, last)
                dve.nop(nofuse=True)
                for t in range(NB):
                    last = dve.bn_aggr(mv[:, t, :], st[:, t, :])
                last.then_inc(stats[which], 1)
                dve.wait_ge(rs_ready[which], b + 1)

            def norm_in(k, b):
                done[k] = 0
                if k == "a":
                    dve.wait_ge(a_in, 16 * b + 16)
                else:
                    dve.wait_ge(res_done["abcd"["abcd".index(k) - 1]], b + 1)
                norm_stats(k, k + "i", b, lambda t: SRC[k][:, t, :])
                for t in range(NB):
                    last = dve.tensor_scalar(xn[:, t, :], SRC[k][:, t, :], mv[:, t, 0:1], rstd[:, t:t + 1],
                                             ALU.subtract, ALU.mult)
                last.then_inc(xn_ready[k], 1)

            def norm_out(k, b, src, into, old, new):
                norm_stats(k, k + "o", b, src)
                for t in range(NB):
                    last = dve.tensor_scalar(into[:, t, :], src(t), mv[:, t, 0:1], rstd[:, t:t + 1],
                                             ALU.subtract, ALU.mult)
                link(k, b, last)
                dve.tensor_tensor(new[:], old[:], into[:], ALU.add).then_inc(res_done[k], 1)
                assert done[k] == CH[k], (k, done[k])

            def a_rotate(b, p):
                dve.wait_ge(a_pair_act, 5 * b + p + 1)
                if p > 0:
                    dve.wait_ge(a_oa, 5 * b + p)
                dve.tensor_tensor(t12[:, 0, :], rab[:, p % 2, 0, :], cos[:], ALU.mult)
                dve.tensor_tensor(t12[:, 1, :], rab[:, p % 2, 1, :], sin[:], ALU.mult).then_inc(a_t12, 1)
                dve.wait_ge(a_t12, 5 * b + p + 1)
                if p >= 2:
                    dve.wait_ge(a_hi, 5 * b + p - 1)
                    dve.wait_ge(a_lo, 5 * b + p - 1)
                dve.tensor_tensor(oab[:, p % 2, 0, :], t12[:, 0, :], t12[:, 1, :], ALU.subtract).then_inc(a_oa, 1)

            def a_low(b, p):
                dve.wait_ge(a_hi, 5 * b + p + 1)
                if p >= 2:
                    dve.wait_ge(a_scr, 160 * b + 32 * (p - 1))
                dve.tensor_tensor(lo[:, p % 2], oab[:, p % 2], hi[:, p % 2].bitcast(F32),
                                  ALU.subtract).then_inc(a_lo, 1)

            def a_main(b):
                for s in range(H0 + 1):
                    if s < H0:
                        for i in range(NB):
                            u = NB * s + i
                            dve.wait_ge(a_s, UNITS * b + u + 1)
                            dve.tensor_reduce(nm[:, u % 8:u % 8 + 1], ps[:, u % 4, 0:P * (i + 1)], AX_X, ALU.max,
                                              negate=True).then_inc(a_nm, 1)
                    if s >= 1:
                        h = s - 1
                        dve.wait_ge(a_tr, H0 * b + h + 1)
                        if h >= 3:
                            dve.wait_ge(a_y_ps, (H0 // 2) * b + (h - 3) // 2 + 1)
                        dve.tensor_copy(ptt[:, h % 3, 0:512], ps[:, 4, :]).then_inc(a_pt_dve, 1)
                    if s < H0:
                        dve.wait_ge(a_exp, UNITS * b + NB * s + NB)
                        link("a", b, dve.reciprocal(rsum[:, s % 2, :], sums[:, s % 2, :]))
                        for i in range(NB):
                            seg = pb[:, s % 2, SEG[i]:SEG[i] + P * (i + 1)]
                            last = dve.tensor_scalar(seg, seg, rsum[:, s % 2, i:i + 1], None, ALU.mult)
                        last.then_inc(a_pn, 1)

            def a_out(b):
                dve.wait_ge(a_o_ps, b + 1)
                norm_out("a", b, lambda t: ps[:, 7, t * P:t * P + P], tmp, x0, x1)

            def c_in(b):
                norm_in("c", b)
                dve.wait_ge(pool_dma, 16 * b + 16)
                dve.tensor_copy(x3[:], x2[:]).then_inc(c_x3, 1)

            def c_split(b):
                dve.wait_ge(c_qk_ps, b + 1)
                qk = ps[:, 0:2, :]
                link("c", b, dve.tensor_copy(parts[:, 0], qk))
                link("c", b, dve.tensor_tensor(res[:], qk, parts[:, 0], ALU.subtract))
                link("c", b, dve.tensor_copy(parts[:, 1], res[:]))
                dve.tensor_tensor(parts[:, 2], res[:], parts[:, 1], ALU.subtract).then_inc(c_parts, 1)

            def c_max(b, u):
                i, h = u // H1, u % H1
                dve.wait_ge(c_s1, 64 * b + u + 1)
                dve.tensor_reduce(nm1[:, i, h:h + 1], ps[:, u % 3, :], AX_X, ALU.max, negate=True).then_inc(c_nm, 1)

            def c_max_split(b):
                dve.wait_ge(c_nm, 64 * b + 64)
                link("c", b, dve.tensor_copy(nmp[:, :, 0, :], nm1[:]))
                link("c", b, dve.tensor_tensor(nm1r[:], nm1[:], nmp[:, :, 0, :], ALU.subtract))
                link("c", b, dve.tensor_copy(nmp[:, :, 1, :], nm1r[:]))
                dve.tensor_tensor(nmp[:, :, 2, :], nm1r[:], nmp[:, :, 1, :], ALU.subtract).then_inc(c_nmp, 1)

            def c_main(b):
                for hg in range(4):
                    dve.wait_ge(c_pv, 16 * b + 4 * hg + 4)
                    dve.tensor_copy(zt[:, hg, :], ps[:, 6 + hg % 2, :]).then_inc(c_z, 1)

            def c_out(b):
                dve.wait_ge(c_zt, b + 1)
                z = ps[:, 4:8, :].rearrange("p b c -> p (b c)").rearrange("p (n d) -> p n d", d=32)
                link("c", b, dve.reciprocal(rc1[:], z[:, :, D1]))
                att = zt[:, 0, :].rearrange("p (t c) -> p t c", c=C)
                dve.tensor_tensor(zt[:, 0, :].rearrange("p (n d) -> p n d", d=D1), z[:, :, 0:D1],
                                  rc1[:].unsqueeze(2).broadcast_to([P, NB * H1, D1]), ALU.mult).then_inc(c_att, 1)
                dve.wait_ge(c_att, b + 1)
                norm_out("c", b, lambda t: att[:, t, :], att, x3, x3)

            def routing(k, b):
                g = FFN[k]
                r = g["routed"]
                lg, eq, oh1, msk, ex, comb = (rt[x][:, :, 0:r] for x in ("lg", "eq", "oh1", "msk", "ex", "comb"))
                rk = ranks[:, 0:r].unsqueeze(1).broadcast_to([P, NB, r])

                def wide(j):
                    return rm[:, j, :].unsqueeze(2).broadcast_to([P, NB, r])

                dve.wait_ge(f_rps[k], b + 1)
                link(k, b, dve.tensor_tensor(lg, ps[:, SBANK, 0:NB * r].rearrange("p (t e) -> p t e", e=r),
                                             g["rb"][:].unsqueeze(1).broadcast_to([P, NB, r]), ALU.add))
                link(k, b, dve.tensor_reduce(rm[:, 0, :], lg, AX_X, ALU.max))
                link(k, b, dve.tensor_tensor(lg, lg, wide(0), ALU.subtract))
                dve.scalar_tensor_tensor(out=eq, in0=lg, scalar=0.0, in1=rk, op0=ALU.is_ge,
                                         op1=ALU.mult).then_inc(f_lm[k], 1)
                dve.wait_ge(f_lm[k], b + 1)
                link(k, b, dve.tensor_reduce(rm[:, 1, :], eq, AX_X, ALU.max))
                link(k, b, dve.tensor_tensor(oh1, eq, wide(1), ALU.is_equal))
                link(k, b, dve.scalar_tensor_tensor(out=msk, in0=oh1, scalar=-BIG, in1=lg,
                                                    op0=ALU.mult, op1=ALU.add))
                link(k, b, dve.tensor_reduce(rm[:, 2, :], msk, AX_X, ALU.max))
                link(k, b, dve.tensor_tensor(eq, msk, wide(2), ALU.is_ge))
                link(k, b, dve.tensor_tensor(eq, eq, rk, ALU.mult))
                link(k, b, dve.tensor_reduce(rm[:, 3, :], eq, AX_X, ALU.max))
                link(k, b, dve.tensor_tensor(msk, eq, wide(3), ALU.is_equal))
                link(k, b, dve.tensor_tensor(msk, msk, oh1, ALU.add))
                dve.wait_ge(f_ex[k], b + 1)
                link(k, b, dve.tensor_tensor(msk, msk, ex, ALU.mult))
                link(k, b, dve.tensor_reduce(rm[:, 0, :], msk if k == "b" else ex, AX_X, ALU.add))
                link(k, b, dve.reciprocal(rm[:, 1, :], rm[:, 0, :]))
                dve.tensor_tensor(comb, msk, wide(1), ALU.mult).then_inc(f_comb[k], 1)

            def piece(k, b, what, e, m):
                n = FFN[k]["n"]
                if what == "bias":
                    dve.wait_ge(f_comb[k], b + 1)
                    dve.wait_ge(f_bias_ps[k], b + 1)
                    dve.tensor_copy(acc[:].rearrange("p t c -> p (t c)"), ps[:, SBANK, :]).then_inc(f_bias[k], 1)
                    dve.wait_ge(f_bias[k], b + 1)
                if what == "down" and m == NB - 1:
                    dve.wait_ge(f_y[k], n * b + e + 1)
                    if e > 0:
                        dve.wait_ge(f_acc[k], n * b + e)
                    for t in range(NB):
                        last = dve.scalar_tensor_tensor(out=acc[:, t, :], in0=ps[:, YBANK, t * P:t * P + P],
                                                        scalar=rt["comb"][:, t, e:e + 1], in1=acc[:, t, :],
                                                        op0=ALU.mult, op1=ALU.add)
                    last.then_inc(f_acc[k], 1)

            def experts_out(k, b):
                dve.wait_ge(f_acc[k], FFN[k]["n"] * b + FFN[k]["n"])
                old, new = (x1, x2) if k == "b" else (x3, x3)
                norm_out(k, b, lambda t: acc[:, t, :], acc, old, new)

            def phase_a(a, d):
                a_rotate(a, 0)
                a_rotate(a, 1)
                a_low(a, 0)
                if d is not None:
                    norm_in("d", d)
                a_rotate(a, 2)
                a_low(a, 1)
                a_rotate(a, 3)
                a_low(a, 2)
                if d is not None:
                    routing("d", d)
                a_rotate(a, 4)
                a_low(a, 3)
                a_low(a, 4)
                if d is not None:
                    for what, e, m in expert_pieces(E1):
                        piece("d", d, what, e, m)
                    experts_out("d", d)
                a_main(a)

            def phase_b(b, c):
                if b is not None:
                    norm_in("b", b)
                c_split(c)
                if b is not None:
                    routing("b", b)
                for what, e, m in interleave(E0 + 1, b is not None):
                    if what == "max":
                        c_max(c, e)
                    elif what == "turn":
                        c_max_split(c)
                    elif what in ("bias", "down"):
                        piece("b", b, what, e, m)
                if b is not None:
                    experts_out("b", b)
                c_main(c)

            dve.memset(rt["comb"][:, :, E0:E0 + 1], 1.0).then_inc(s_comb1, 1)
            dve.wait_ge(s_comb1, 1)
            dve.wait_ge(s_const, 3 + E0)
            dve.wait_ge(pool_dma, 16)
            dve.wait_ge(s_w, 16 * NWA)
            norm_in("a", 0)
            phase_a(0, None)
            a_out(0)
            dve.wait_ge(s_wf, 16 * NWF)
            norm_in("b", 0)
            routing("b", 0)
            for what, e, m in expert_pieces(E0 + 1):
                piece("b", 0, what, e, m)
            experts_out("b", 0)
            norm_in("a", 1)
            phase_a(1, None)
            with dve.Fori(1, NSEQ - 1) as i:
                c_in(i - 1)
                a_out(i)
                phase_b(i, i - 1)
                norm_in("a", i + 1)
                c_out(i - 1)
                phase_a(i + 1, i - 1)
            c_in(NSEQ - 2)
            a_out(NSEQ - 1)
            phase_b(NSEQ - 1, NSEQ - 2)
            for n in (NSEQ - 2, NSEQ - 1):
                c_out(n)
                norm_in("d", n)
                routing("d", n)
                for what, e, m in expert_pieces(E1):
                    piece("d", n, what, e, m)
                experts_out("d", n)
                if n == NSEQ - 2:
                    c_in(n + 1)
                    phase_b(None, n + 1)

def kernel(**inputs):
    import numpy as np
    import concourse.bacc as bacc
    from concourse.bass_utils import run_bass_kernel_spmd

    v = {k: np.asarray(a) for k, a in inputs.items()}

    def blocks(w):
        return w.reshape(-1, P, w.shape[-1]).transpose(1, 0, 2)

    wq = v["L0_attn_Wq"].reshape(C, NG, 4, HALF, 2)
    wk = v["L0_attn_Wk"].reshape(C, KV0, HALF, 2)
    w1 = np.concatenate([v["L0_ffn_spec_w1"], v["L0_ffn_shared_w1"][None]])
    b1 = np.concatenate([v["L0_ffn_spec_b1"], v["L0_ffn_shared_b1"][None]])
    w2 = np.concatenate([v["L0_ffn_spec_w2"], v["L0_ffn_shared_w2"][None]])
    b2 = np.concatenate([v["L0_ffn_spec_b2"], v["L0_ffn_shared_b2"][None]])
    f32 = np.float32
    inv_freq = f32(1.0) / f32(10000.0) ** (np.arange(0, D0, 2, dtype=f32) / f32(D0))
    angle = (np.arange(T, dtype=f32)[None, :] * inv_freq[:, None]).astype(f32)
    bf16 = mybir.dt.np(BF16)
    arrays = {
        "x": v["L0_attn_x"].reshape(NSEQ, NB, P, C).transpose(0, 2, 1, 3),
        "wqa": wq[..., 0].reshape(C, NG, P), "wqb": wq[..., 1].reshape(C, NG, P),
        "wka": wk[..., 0].reshape(C, P), "wkb": wk[..., 1].reshape(C, P),
        "wv0": v["L0_attn_Wv"], "wo": blocks(v["L0_attn_Wo"]),
        "cos": np.tile(np.cos(angle), (4, 1)), "sin": np.tile(np.sin(angle), (4, 1)),
        "ident": np.eye(P, dtype=f32), "identb": np.eye(P, dtype=f32).astype(bf16),
        "maskb": np.triu(np.full((P, P), -BIG, f32), 1).astype(bf16),
        "f0w1": w1.transpose(2, 0, 1), "f0b1": b1.reshape(E0 + 1, NF, P).transpose(2, 0, 1),
        "f0w2": w2.transpose(2, 0, 1).reshape(NF, P, E0 + 1, C).transpose(1, 2, 0, 3), "f0b2": b2,
        "r0w": v["L0_ffn_router_w"].T, "r0b": np.broadcast_to(v["L0_ffn_router_b"], (P, E0)),
        "w1q": v["L1_attn_w_Q"], "w1k": v["L1_attn_w_K"], "w1v": v["L1_attn_w_V"],
        "f1w1": v["L1_ffn_We1"].transpose(1, 0, 2), "f1b1": v["L1_ffn_be1"].reshape(E1, NF, P).transpose(2, 0, 1),
        "f1w2": v["L1_ffn_We2"].reshape(E1, NF, P, C).transpose(2, 0, 1, 3), "f1b2": v["L1_ffn_be2"],
        "r1w1": v["L1_ffn_rW1"], "r1b1": v["L1_ffn_rb1"].reshape(2, P).T,
        "r1w2": blocks(v["L1_ffn_rW2"]), "r1b2": np.broadcast_to(v["L1_ffn_rb2"], (P, E1)),
    }
    nc = bacc.Bacc("TRN2", target_bir_lowering=False, num_devices=1)
    arrays = {k: np.ascontiguousarray(a) for k, a in arrays.items()}
    io = {k: nc.dram_tensor(k, a.shape, mybir.dt.from_np(a.dtype), kind="ExternalInput").ap()
          for k, a in arrays.items()}
    io["out"] = nc.dram_tensor("out", (NSEQ, P, NB, C), F32, kind="ExternalOutput").ap()
    sandwich_kernel(nc, io)
    r = run_bass_kernel_spmd(nc, [arrays], core_ids=[0])
    return r.results[0]["out"].transpose(0, 2, 1, 3).reshape(NSEQ, T, C)
```

```python
import math
from contextlib import ExitStack

import concourse.bass as bass
from concourse import mybir
from concourse.alu_op_type import AluOpType as ALU

ACT = mybir.ActivationFunctionType
F32 = mybir.dt.float32
F32R = mybir.dt.float32r
BF16 = mybir.dt.bfloat16
AX_X = mybir.AxisListType.X

P = 128
NSEQ, T, C = 8, 512, 128
NB = T // P
H0, KV0, D0 = 16, 4, 64
HALF = D0 // 2
NG = H0 // 4
H1, D1 = 16, 8
E0, E1 = 8, 4
FF = 512
NF = FF // P
EPS = 1e-5
BIG = 1e30
UNITS = H0 * NB
SEG = [P * (i * (i + 1) // 2) for i in range(NB)]
HEADW = P * NB * (NB + 1) // 2
TSEG = [0, 512, 1024, 896]
TBANK = [(4, 0), (5, 0), (6, 0), (5, 384)]
ROWS1 = 9 * D1
MROW = 96
ONES = 1 + 0x3F80 * 2.0 ** -23
SC1 = float(D1) ** -0.5
KSTACK_DMAS, QSTACK_DMAS = 8, 4
RHBANK = 5
HALVES = (slice(0, NB // 2), slice(NB // 2, NB))
RING = 3
PAIRBANK = [0, 6, 4, 0, 0]
YBANK, YLAST = 7, 6
SBANK = 3
QKBANK, VBANK = 0, 2


def expert_pieces(n):
    ups = {e: [("up", e, f) for f in range(NF)] for e in range(n)}
    downs = {e: [("down", e, t) for t in range(NB)] for e in range(n)}
    order = ups[0] + ups[1]
    order += downs[0][:-1] + [("weights", 0, 0)] + ups[2][:1] + [("bias", 0, 0)] + downs[0][-1:] + ups[2][1:]
    for e in range(1, n):
        order += downs[e]
        if e + 2 < n:
            order += ups[e + 2]
    return order


def beside_attention(k, n):
    pieces = expert_pieces(n)
    after = [p for p in pieces if k == "d" and p[1] == n - 1 and p[0] in ("up", "down")]
    return [p for p in pieces if p not in after], after


def interleave(n):
    pieces = expert_pieces(n)
    first = min(2 * NF + 3 * NB + 1, len(pieces) // 2)
    head, body, tail = pieces[:first], pieces[first:-2 * NB], pieces[-2 * NB:]
    order, used = head + [("stack", 0, 0)], 0
    for u in range(4 * H1):
        order.append(("max", u, 0))
        while used < len(body) * (u + 1) // (4 * H1):
            order.append(body[used])
            used += 1
    return order + [("split", 0, 0)] + tail[:NB // 2] + [("turn", 0, 0)] + tail[NB // 2:]


def sandwich_kernel(nc, io):
    with ExitStack() as ctx:
        base = (nc.sbuf_base + 63) // 64 * 64
        top = [base]

        def size(shape, dt):
            n = 2 if dt == BF16 else 4
            for s in shape[1:]:
                n *= s
            return (n + 31) // 32 * 32

        def sb(name, shape, dt=F32):
            t = nc.alloc_sbuf_tensor_at(name, shape, dt, offset=top[0])
            top[0] += size(shape, dt)
            return t

        def region(kib):
            at = top[0]
            top[0] += kib * 1024
            return [at, at + kib * 1024]

        def sub(reg, name, shape, dt=F32):
            t = nc.alloc_sbuf_tensor_at(name, shape, dt, offset=reg[0])
            reg[0] += size(shape, dt)
            assert reg[0] <= reg[1], name
            return t

        def sem(name):
            return ctx.enter_context(nc.semaphore(name))

        ps = ctx.enter_context(nc.psum_tensor("ps", [P, 8, 512], F32))

        wqa, wqb = sb("wqa", [P, NG, P]), sb("wqb", [P, NG, P])
        wka, wkb = sb("wka", [P, P]), sb("wkb", [P, P])
        wv0 = sb("wv0", [P, KV0 * D0])
        wo = sb("wo", [P, H0 * D0 // P, C])
        cos, sin = sb("cos", [P, T]), sb("sin", [P, T])
        ident, identb, maskb = sb("ident", [P, P]), sb("identb", [P, P], BF16), sb("maskb", [P, P], BF16)
        f0w1, f0b1 = sb("f0w1", [P, E0 + 1, FF]), sb("f0b1", [P, E0 + 1, NF])
        f0w2, f0b2 = sb("f0w2", [P, E0 + 1, NF, C]), sb("f0b2", [E0 + 1, C])
        r0w, r0b = sb("r0w", [P, E0]), sb("r0b", [P, E0])
        w1q, w1k, w1v = sb("w1q", [P, P]), sb("w1k", [P, P]), sb("w1v", [P, P])
        f1w1, f1b1 = sb("f1w1", [P, E1, FF]), sb("f1b1", [P, E1, NF])
        f1w2, f1b2 = sb("f1w2", [P, E1, NF, C]), sb("f1b2", [E1, C])
        r1w1, r1b1 = sb("r1w1", [P, 2 * P]), sb("r1b1", [P, 2])
        r1w2, r1b2 = sb("r1w2", [P, 2, E1]), sb("r1b2", [P, E1])
        ranks = sb("ranks", [P, E0])
        neghalf = sb("neghalf", [P, NB])
        euler = sb("euler", [P, NB * E0])
        x0, x1, x2, x3 = (sb(f"x{i}", [P, NB, C]) for i in range(4))
        xn = sb("xn", [P, NB, C])
        xta, xtb = sb("xta", [P, T]), sb("xtb", [P, T])
        st, mv, rstd = sb("st", [P, NB, 6]), sb("mv", [P, NB, 2]), sb("rstd", [P, NB])
        acc = sb("acc", [P, NB, C])
        r_q = region(32)
        qs = nc.alloc_sbuf_tensor_at("qs", [P, H0, T], F32R, offset=r_q[0])
        pt1 = sub(r_q, "pt1", [P, 4, 2, T])
        zt = sub(r_q, "zt", [P, 4, T])
        parts = sub(r_q, "parts", [P, 3, 2, T], BF16)
        r_k = region(16)
        ks1 = nc.alloc_sbuf_tensor_at("ks1", [P, KV0, T], F32R, offset=r_k[0])
        ks2 = nc.alloc_sbuf_tensor_at("ks2", [P, KV0, T], F32R, offset=r_k[0] + 8192)
        qd = sub(r_k, "qd", [P, H1, T], BF16)
        r_h = region(16)
        hi = nc.alloc_sbuf_tensor_at("hi", [P, 2, 2, T], F32R, offset=r_h[0])
        lo = nc.alloc_sbuf_tensor_at("lo", [P, 2, 2, T], F32R, offset=r_h[0] + 8192)
        kd = sub(r_h, "kd", [P, H1, T], BF16)
        r_t = region(16)
        hid0 = nc.alloc_sbuf_tensor_at("hid0", [P, NF, T], F32, offset=r_t[0] + 8192)
        yt = nc.alloc_sbuf_tensor_at("yt", [P, H0 // 2, T], F32, offset=r_t[0])
        tmp = nc.alloc_sbuf_tensor_at("tmp", [P, NB, C], F32, offset=r_t[0])
        t12 = sub(r_t, "t12", [P, 2, T])
        t34 = sub(r_t, "t34", [P, 2, T])
        r_p = region(25)
        hid = [hid0,
               nc.alloc_sbuf_tensor_at("hid1", [P, NF, T], F32, offset=r_p[0] + 16384)]
        rh = nc.alloc_sbuf_tensor_at("rh", [P, 2, T], F32, offset=r_p[0] + 16384)
        rab = nc.alloc_sbuf_tensor_at("rab", [P, 2, 2, T], F32, offset=r_p[0])
        oab = nc.alloc_sbuf_tensor_at("oab", [P, 2, 2, T], F32, offset=r_p[0] + 8192)
        pb = sub(r_p, "pb", [P, 2, HEADW])
        ptt = sub(r_p, "ptt", [P, 3, HEADW])
        r_v = region(4)
        v0 = nc.alloc_sbuf_tensor_at("v0", [P, NB, KV0 * D0], F32, offset=r_v[0])
        res = sub(r_v, "res", [P, 2, T])
        vs = sb("vs", [P, NB, H1, 32])
        combt = nc.alloc_sbuf_tensor_at("combt", [E0 + 1, T], F32, offset=top[0])
        mt = nc.alloc_sbuf_tensor_at("mt", [48, T], BF16, offset=top[0])
        top[0] += 4 * T
        nm = sb("nm", [P, 8])
        sums, rsum = sb("sums", [P, 2, NB]), sb("rsum", [P, 2, NB])
        r_s = [top[0], top[0] + 1152]
        rt = {k: nc.alloc_sbuf_tensor_at("rt_" + k, [P, NB, E0 + 1], F32, offset=r_s[0] + 160 * n)
              for n, k in enumerate(("lg", "eq", "oh1", "msk", "ex"))}
        nm1, nm1r = sub(r_s, "nm1", [P, NB, H1]), sub(r_s, "nm1r", [P, NB, H1])
        nmp = sub(r_s, "nmp", [P, NB, 3, H1], BF16)
        rc1 = sub(r_s, "rc1", [P, NB * H1])
        top[0] += 1152
        rt["comb"] = sb("comb", [P, NB, E0 + 1])
        rm = sb("rm", [P, 4, NB])
        assert top[0] <= nc.sbuf_usable_end, (top[0], nc.sbuf_usable_end)

        rotated = nc.dram_tensor("rotated", [1 + NG, 2, P, 2, T], F32).ap()
        scratch = nc.dram_tensor("scratch", [2, 3, P, T], BF16).ap()

        s_w = sem("s_w"); s_comb1 = sem("s_comb1"); s_const = sem("s_const"); s_wscaled = sem("s_wscaled")
        s_wf = sem("s_wf"); s_ident = sem("s_ident")
        a_in = sem("a_in")
        stats = {k: sem("stats_" + k) for k in ("ai", "ao", "bi", "bo", "ci", "co", "di", "do")}
        rs_ready = {k: sem("rs_" + k) for k in ("ai", "ao", "bi", "bo", "ci", "co", "di", "do")}
        xn_ready = {k: sem("xn_" + k) for k in "abcd"}
        xt_ps = {k: sem("xtps_" + k) for k in "abcd"}
        xt_ready = {k: sem("xt_" + k) for k in "abcd"}
        res_done = {k: sem("res_" + k) for k in "abcd"}
        chain = {k: sem("chain_" + k) for k in "abcdz"}
        pch = {k: sem("pch_" + k) for k in ("ai", "ao", "bi", "bo", "ci", "co", "di", "do", "rope")}
        a_pair_ps = sem("a_pair_ps"); a_pair_act = sem("a_pair_act"); a_t12 = sem("a_t12")
        a_oa = sem("a_oa"); a_ob = sem("a_ob"); a_hi = sem("a_hi"); a_lo = sem("a_lo")
        a_v_ps = sem("a_v_ps"); a_v = sem("a_v")
        a_scr = sem("a_scr")
        a_kst = sem("a_kst"); a_qst = [sem(f"a_qst{g}") for g in range(NG)]
        a_s = sem("a_s"); a_nm = sem("a_nm"); a_exp = sem("a_exp")
        a_rs = sem("a_rs"); a_pn = sem("a_pn"); a_tr = sem("a_tr"); a_pt = sem("a_pt")
        a_y_ps = sem("a_y_ps"); a_yt = sem("a_yt")
        a_pt_first = sem("a_pt_first")
        a_o_ps = sem("a_o_ps")
        c_qk_ps = sem("c_qk_ps"); c_v_ps = sem("c_v_ps"); c_v = sem("c_v")
        c_res = sem("c_res"); c_parts = sem("c_parts")
        c_scr = sem("c_scr"); c_stack = sem("c_stack"); c_pad = sem("c_pad")
        c_s1 = sem("c_s1"); c_nm = sem("c_nm")
        c_nmp = sem("c_nmp"); c_mt_ps = sem("c_mt_ps"); c_mt = sem("c_mt"); c_mrow = sem("c_mrow")
        c_s2 = sem("c_s2"); c_exp = sem("c_exp")
        c_pv = sem("c_pv"); c_z = sem("c_z")
        c_x3 = sem("c_x3"); c_zt = sem("c_zt"); c_att = sem("c_att")
        f_rps = {k: sem("rps_" + k) for k in "bd"}; f_lm = {k: sem("lm_" + k) for k in "bd"}
        f_ex = {k: sem("ex_" + k) for k in "bd"}; f_comb = {k: sem("comb_" + k) for k in "bd"}
        f_ctps = {k: sem("ctps_" + k) for k in "bd"}; f_ct = {k: sem("ct_" + k) for k in "bd"}
        f_bias_ps = {k: sem("biasps_" + k) for k in "bd"}; f_bias = {k: sem("bias_" + k) for k in "bd"}
        f_h = {k: sem("h_" + k) for k in "bd"}; f_g = {k: sem("g_" + k) for k in "bd"}
        f_y = {k: sem("y_" + k) for k in "bd"}; f_acc = {k: sem("acc_" + k) for k in "bd"}
        d_rh_ps = sem("d_rh_ps"); d_rh = sem("d_rh")
        pool_dma = sem("pool_dma")

        SRC = {"a": x0, "b": x1, "c": x2, "d": x3}
        FFN = {"b": dict(n=E0 + 1, routed=E0, w1=f0w1, b1=f0b1, w2=f0w2, b2=f0b2, rb=r0b),
               "d": dict(n=E1, routed=E1, w1=f1w1, b1=f1b1, w2=f1w2, b2=f1b2, rb=r1b2)}

        def xt_bank(k, b):
            if k == "a" or k == "c" and isinstance(b, int) and b == NSEQ - 1:
                return 5
            return YBANK if k == "c" else SBANK

        def xt_tile(k, b):
            return xtb if k in ("c", "d") or isinstance(b, int) and b == 0 and k == "b" else xta

        def y_bank(k, b, e):
            n = FFN[k]["n"]
            parted = k == "d" and not isinstance(b, int)
            return YLAST if e == n - 1 or parted and e == n - 2 else YBANK

        FIRST = (("wka", wka), ("wkb", wkb), ("wv0", wv0), ("cos", cos), ("sin", sin),
                 ("wqa", wqa), ("wqb", wqb), ("identb", identb), ("maskb", maskb))
        LATER = (("wo", wo), ("r0w", r0w), ("r0b", r0b), ("f0b1", f0b1), ("f0b2", f0b2),
                 ("f0w1", f0w1), ("f0w2", f0w2), ("w1q", w1q), ("w1k", w1k), ("w1v", w1v),
                 ("r1w1", r1w1), ("r1b1", r1b1), ("r1w2", r1w2),
                 ("f1b1", f1b1), ("f1b2", f1b2), ("f1w1", f1w1), ("f1w2", f1w2))
        x_dram, out_dram = io["x"], io["out"]
        block = ctx.enter_context(nc.Block())


        @block.sync
        def _(sp):
            sp.dma_start(x0[:], x_dram[0]).then_inc(a_in, 16)
            sp.dma_start(ident[:], io["ident"]).then_inc(s_ident, 16)
            for name, dst in FIRST:
                sp.dma_start(dst[:], io[name]).then_inc(s_w, 16)

            def a_rope(b):
                if not (isinstance(b, int) and b == 0):
                    sp.wait_ge(res_done["a"], b)
                    sp.dma_start(x0[:], x_dram[b]).then_inc(a_in, 16)
                for p in range(1 + NG):
                    sp.wait_ge(a_hi, 5 * b + p + 1)
                    sp.dma_start(rotated[p, 0], hi[:, p % 2].bitcast(F32)).then_inc(a_scr, 16)
                    sp.wait_ge(a_lo, 5 * b + p + 1)
                    sp.dma_start(rotated[p, 1], lo[:, p % 2].bitcast(F32)).then_inc(a_scr, 16)
                    sp.wait_ge(a_scr, 160 * b + 32 * p + 32)
                    for r in range(4):
                        src = rotated[p, r // 2, :, r % 2, :].rearrange("(h j) t -> j h t", j=HALF)
                        rows = slice(HALF * r, HALF * r + HALF)
                        if p == 0:
                            swapped = slice(HALF * ((r + 2) % 4), HALF * ((r + 2) % 4) + HALF)
                            sp.dma_start(ks1[rows, :, :].bitcast(F32), src).then_inc(a_kst, 16)
                            sp.dma_start(ks2[swapped, :, :].bitcast(F32), src).then_inc(a_kst, 16)
                        else:
                            sp.dma_start(qs[rows, 4 * (p - 1):4 * p, :].bitcast(F32), src).then_inc(a_qst[p - 1], 16)

            def c_main(b):
                sp.wait_ge(c_parts, b + 1)
                for w in range(2):
                    sp.dma_start(scratch[w].rearrange("s p t -> p s t"), parts[:, :, w, :]).then_inc(c_scr, 16)
                sp.wait_ge(c_scr, 32 * b + 32)
                sp.wait_ge(c_pad, 3 * b + 3)
                for s in range(3):
                    for s2 in range(3):
                        r = (3 * s + s2) * D1
                        sp.dma_start(qd[r:r + D1, :, :],
                                     scratch[0, s].rearrange("(h d) t -> d h t", d=D1)).then_inc(c_stack, 16)
                        sp.dma_start(kd[r:r + D1, :, :],
                                     scratch[1, s2].rearrange("(h d) t -> d h t", d=D1)).then_inc(c_stack, 16)
                sp.wait_ge(c_mt, b + 1)
                for s in range(3):
                    sp.dma_start(qd[MROW + s:MROW + s + 1, :, :], mt[16 * s:16 * s + 16, :]).then_inc(c_mrow, 16)

            a_rope(0)
            for name, dst in LATER:
                sp.dma_start(dst[:], io[name]).then_inc(s_wf, 16)
            a_rope(1)
            with sp.Fori(1, NSEQ - 1) as i:
                c_main(i - 1)
                a_rope(i + 1)
            c_main(NSEQ - 2)
            c_main(NSEQ - 1)

        @block.gpsimd
        def _(pool):
            pool.memset(neghalf[:], -0.5).then_inc(s_const, 1)
            pool.memset(vs[:], 0.0).then_inc(s_const, 1)
            pool.dma_start(r1b2[:], io["r1b2"]).then_inc(pool_dma, 16)
            pool.wait_ge(s_const, 2)
            pool.memset(vs[:, :, :, D1:D1 + 1], 1.0).then_inc(s_const, 1)
            pool.memset(euler[:], math.e).then_inc(s_const, 1)
            for e in range(E0):
                pool.memset(ranks[:, e:e + 1], float(E0 - e)).then_inc(s_const, 1)
            pool.wait_ge(s_const, 4 + E0)

            def norm_scale(which, b):
                for h, half in enumerate(HALVES):
                    pool.wait_ge(stats[which], 2 * b + h + 1)
                    pool.nop(nofuse=True)
                    pool.tensor_scalar(rstd[:, half], mv[:, half, 1], EPS, None, ALU.add).then_inc(pch[which], 1)
                    pool.wait_ge(pch[which], 2 * b + h + 1)
                    pool.tensor_tensor(rstd[:, half], rstd[:, half], neghalf[:, half],
                                       ALU.pow).then_inc(rs_ready[which], 1)

            def a_rope(b, start, end):
                for p in range(start, end):
                    pool.wait_ge(a_pair_act, 5 * b + p + 1)
                    if p > 0:
                        pool.wait_ge(a_ob, 5 * b + p)
                    pool.tensor_tensor(t34[:, 0, :], rab[:, p % 2, 0, :], sin[:], ALU.mult)
                    pool.tensor_tensor(t34[:, 1, :], rab[:, p % 2, 1, :], cos[:], ALU.mult).then_inc(pch["rope"], 1)
                    pool.wait_ge(pch["rope"], 5 * b + p + 1)
                    if p > 1:
                        pool.wait_ge(a_hi, 5 * b + p - 1)
                        pool.wait_ge(a_lo, 5 * b + p - 1)
                    pool.tensor_tensor(oab[:, p % 2, 1, :], t34[:, 0, :], t34[:, 1, :], ALU.add).then_inc(a_ob, 1)

            def c_pads(b):
                pool.nop(nofuse=True)
                pool.memset(qd[64:P, :, :].bitcast(F32), 0.0).then_inc(c_pad, 1)
                pool.wait_ge(c_pad, 3 * b + 1)
                pool.nop(nofuse=True)
                pool.memset(kd[64:MROW, :, :].bitcast(F32), 0.0).then_inc(c_pad, 1)
                pool.wait_ge(c_pad, 3 * b + 2)
                pool.nop(nofuse=True)
                pool.memset(kd[MROW:P, :, :].bitcast(F32), ONES).then_inc(c_pad, 1)
                pool.wait_ge(c_pad, 3 * b + 3)
                pool.nop(nofuse=True)

            def c_residual(b):
                pool.wait_ge(pool_dma, 16 * b + 16)
                pool.wait_ge(res_done["b"], b + 1)
                pool.nop(nofuse=True)
                pool.tensor_copy(x3[:], x2[:]).then_inc(c_x3, 1)

            def out(b):
                pool.wait_ge(res_done["d"], b + 1)
                pool.dma_start(out_dram[b], x3[:]).then_inc(pool_dma, 16)

            def routing(k, b):
                r = FFN[k]["routed"]
                pool.wait_ge(f_lm[k], b + 1)
                if k == "b":
                    pool.tensor_tensor(rt["ex"][:, 0, 0:NB], euler[:, 0:NB], rm[:, 2, :],
                                       ALU.pow).then_inc(f_ex[k], 1)
                    return
                pool.tensor_tensor(rt["ex"][:, :, 0:r], euler[:, 0:NB * r].rearrange("p (t e) -> p t e", e=r),
                                   rt["lg"][:, :, 0:r], ALU.pow).then_inc(f_ex[k], 1)

            def bridge(a, d):
                norm_scale("ao", a)
                norm_scale("bi", a)
                if d is not None:
                    norm_scale("do", d)
                routing("b", a)
                if d is not None:
                    out(d)

            def phase_a(a, k, n, c):
                a_rope(a, 0, 1)
                norm_scale(k + "i", n)
                a_rope(a, 1, 3)
                routing(k, n)
                a_rope(a, 3, 1 + NG)
                if k == "b":
                    norm_scale("bo", n)
                norm_scale("ci", c)
                pool.wait_ge(a_s, UNITS * a + UNITS)
                pool.wait_ge(rs_ready["ci"], 2 * c + 2)
                c_pads(c)

            norm_scale("ai", 0)
            pool.wait_ge(s_w, 16 * len(FIRST))
            a_rope(0, 0, 1 + NG)
            norm_scale("ao", 0)
            norm_scale("ai", 1)
            phase_a(1, "b", 0, 0)
            bridge(1, None)
            with pool.Fori(1, NSEQ - 1) as i:
                c_residual(i - 1)
                norm_scale("bo", i)
                norm_scale("ai", i + 1)
                norm_scale("co", i - 1)
                phase_a(i + 1, "d", i - 1, i)
                bridge(i + 1, i - 1)
            last = NSEQ - 1
            c_residual(last - 1)
            norm_scale("bo", last)
            norm_scale("ci", last)
            norm_scale("co", last - 1)
            norm_scale("di", last - 1)
            pool.wait_ge(rs_ready["di"], 2 * last)
            c_pads(last)
            routing("d", last - 1)
            norm_scale("do", last - 1)
            out(last - 1)
            c_residual(last)
            norm_scale("co", last)
            norm_scale("di", last)
            routing("d", last)
            norm_scale("do", last)
            out(last)
            pool.wait_ge(pool_dma, 16 * (NSEQ + 1))

        @block.tensor
        def _(pe):
            def to_channels(k, b):
                for t in range(NB):
                    if t % 2 == 0:
                        pe.wait_ge(xn_ready[k], 2 * b + t // 2 + 1)
                    last = pe.transpose(ps[:, xt_bank(k, b), t * P:t * P + P], xn[:, t, :], ident[:])
                last.then_inc(xt_ps[k], 1)

            def a_pair(b, p, between=None):
                if p == 0:
                    pe.wait_ge(xt_ready["a"], b + 1)
                if p >= 3:
                    pe.wait_ge(a_pair_act, 5 * b + (1 if p == 3 else 4))
                if p == 1 and isinstance(b, int):
                    pe.wait_ge(s_wscaled, 2)
                pe.matmul(ps[:, PAIRBANK[p], :], wka[:] if p == 0 else wqa[:, p - 1, :], xta[:], start=True, stop=True)
                if between is not None:
                    to_channels(*between)
                pe.matmul(ps[:, PAIRBANK[p] + 1, :], wkb[:] if p == 0 else wqb[:, p - 1, :], xta[:], start=True,
                          stop=True).then_inc(a_pair_ps, 1)
                if p < 2:
                    if p == 1:
                        pe.wait_ge(a_v, 2 * b + 1)
                    for t in range(2 * p, 2 * p + 2):
                        last = pe.matmul(ps[:, 2, 256 * (t % 2):256 * (t % 2) + 256],
                                         xta[:, t * P:t * P + P], wv0[:], start=True, stop=True)
                    last.then_inc(a_v_ps, 1)

            def a_scores(b, h):
                if h == 0:
                    pe.wait_ge(a_pair_act, 5 * b + 5)
                    pe.wait_ge(a_v, 2 * b + 2)
                    pe.wait_ge(a_kst, 16 * KSTACK_DMAS * b + 16 * KSTACK_DMAS)
                if h % 4 == 0:
                    pe.wait_ge(a_qst[h // 4], 16 * QSTACK_DMAS * b + 16 * QSTACK_DMAS)
                for i in range(NB):
                    u = NB * h + i
                    n = P * (i + 1)
                    if u >= 4:
                        pe.wait_ge(a_exp, UNITS * b + u - 3)
                    q = qs[:, h, P * i:P * i + P]
                    s = ps[:, u % 4, 0:n]
                    pe.matmul(ps[:, u % 4, n - P:n], identb[:], maskb[:], start=True, stop=False,
                              skip_group_check=True)
                    pe.matmul(s, q, ks1[:, h // 4, 0:n], start=False, stop=False, skip_group_check=True)
                    pe.matmul(s, q, ks2[:, h // 4, 0:n], start=False, stop=True,
                              skip_group_check=True).then_inc(a_s, 1)

            def a_main(b, k=None, n=None):
                def transposes(h):
                    pe.wait_ge(a_pn, H0 * b + h + 1)
                    if h > 0:
                        pe.wait_ge(a_pt, H0 * b + h)
                    for i in range(NB):
                        for kb in range(i + 1):
                            bank, col = TBANK[kb]
                            col += P * (i - kb)
                            last = pe.transpose(ps[:, bank, col:col + P],
                                                pb[:, h % 2, SEG[i] + P * kb:SEG[i] + P * kb + P], ident[:])
                    last.then_inc(a_tr, 1)

                def weighted_values(j, blocks):
                    kv = j // 2
                    for kb in blocks:
                        for s in range(2):
                            n = T - P * kb
                            last = pe.matmul(ps[64 * s:64 * s + 64, 7, P * kb:T],
                                             v0[:, kb, D0 * kv:D0 * kv + D0],
                                             ptt[:, (2 * j + s) % 3, TSEG[kb]:TSEG[kb] + n],
                                             start=(kb == 0), stop=(kb == 2), skip_group_check=True)
                    return last

                def project(pairs):
                    for t in range(NB):
                        for j in pairs:
                            last = pe.matmul(ps[:, t, 0:C], yt[:, j, t * P:t * P + P], wo[:, j, :],
                                             start=(j == 0), stop=(j == H0 // 2 - 1), skip_group_check=True)
                        if j == H0 // 2 - 1:
                            last.then_inc(a_o_ps, 1)

                for s in range(1, H0 + 3):
                    if s < H0:
                        a_scores(b, s)
                    j = (s - 3) // 2
                    if s >= 3 and s % 2:
                        pe.wait_ge(a_pt, H0 * b + 2 * j + 1)
                        pe.wait_ge(a_pt_first, (H0 // 2) * b + j + 1)
                        if j > 0:
                            pe.wait_ge(a_yt, (H0 // 2) * b + j)
                        weighted_values(j, (0, 3))
                    if s >= 3 and s % 2 == 0:
                        pe.wait_ge(a_pt, H0 * b + 2 * j + 2)
                        weighted_values(j, (1, 2)).then_inc(a_y_ps, 1)
                    if s == 1 and k is not None:
                        experts = FFN[k]["n"]
                        pe.wait_ge(f_acc[k], experts * n + (experts - 1 if k == "d" else experts))
                    if s == H0:
                        if isinstance(b, int) and b == 0:
                            pe.wait_ge(s_wf, 16 * len(LATER))
                        pe.wait_ge(a_exp, UNITS * b + UNITS)
                        project(range(2))
                    if s <= H0:
                        transposes(s - 1)
                    if s == H0:
                        pe.wait_ge(a_yt, (H0 // 2) * b + H0 // 2 - 2)
                        project(range(2, H0 // 2 - 2))
                    if s == H0 + 1:
                        pe.wait_ge(a_yt, (H0 // 2) * b + H0 // 2 - 1)
                project((H0 // 2 - 2,))
                pe.wait_ge(a_yt, (H0 // 2) * b + H0 // 2)
                project((H0 // 2 - 1,))

            def c_project(b):
                pe.wait_ge(xt_ready["c"], b + 1)
                pe.matmul(ps[:, QKBANK, :], w1q[:], xtb[:], start=True, stop=True)

            def c_project_keys(b):
                pe.matmul(ps[:, QKBANK + 1, :], w1k[:], xtb[:], start=True, stop=True).then_inc(c_qk_ps, 1)

            def c_project_values(b):
                for t in range(NB):
                    last = pe.matmul(ps[:, VBANK, t * P:t * P + P], xtb[:, t * P:t * P + P], w1v[:],
                                     start=True, stop=True)
                last.then_inc(c_v_ps, 1)

            def c_max_scores(b, u):
                i, h = u // H1, u % H1
                if u >= 3:
                    pe.wait_ge(c_nm, 64 * b + u - 2)
                pe.matmul(ps[:, u % 3, :], qd[:, h, i * P:i * P + P], kd[:, h, :], start=True,
                          stop=True).then_inc(c_s1, 1)

            def c_turn(b):
                pe.wait_ge(c_nmp, b + 1)
                pe.nop(nofuse=True)
                mtp = ps[0:48, SBANK, 0:T // 2].bitcast(BF16)
                for t in range(NB):
                    last = pe.transpose(mtp[:, t * P:t * P + P],
                                        nmp[:, t, :, :].rearrange("p s h -> p (s h)"), identb[:])
                last.then_inc(c_mt_ps, 1)

            def c_main(b, k, n, following):
                pe.wait_ge(c_mrow, 48 * b + 48)

                def scores(w):
                    hg, kb, gp = w // 8, (w // 2) % 4, w % 2
                    if w >= 3:
                        pe.wait_ge(c_exp, 32 * b + w - 2)
                    for g in range(2):
                        h = 4 * hg + 2 * gp + g
                        last = pe.matmul(ps[:, 2 * (w % 3) + g, :], kd[:, h, kb * P:kb * P + P], qd[:, h, :],
                                         start=True, stop=True)
                    last.then_inc(c_s2, 1)

                def weighted_values(y):
                    hg, kb = y // 4, y % 4
                    pe.wait_ge(c_exp, 32 * b + 2 * y + 2)
                    if kb == 0 and hg == 0:
                        pe.wait_ge(f_acc[k], FFN[k]["n"] * n + FFN[k]["n"])
                    if kb == 0 and hg >= 2:
                        pe.wait_ge(c_z, 4 * b + hg - 1)
                    for g in range(4):
                        last = pe.matmul(ps[32 * g:32 * g + 32, 6 + hg % 2, :], vs[:, kb, 4 * hg + g, :],
                                         pt1[:, (2 * y + g // 2) % 4, g % 2, :],
                                         start=(kb == 0), stop=(kb == NB - 1), skip_group_check=True)
                    last.then_inc(c_pv, 1)

                for y in range(16 + 1):
                    if y < 16:
                        scores(2 * y)
                        scores(2 * y + 1)
                    if y == 16 and following is not None:
                        pe.wait_ge(c_exp, 32 * b + 30)
                        to_channels(*following)
                    if y >= 1:
                        weighted_values(y - 1)

            def c_out(b):
                pe.wait_ge(c_z, 4 * b + 4)
                for i in range(NB):
                    for hg in range(4):
                        last = pe.transpose(ps[:, 4 + i, hg * P:hg * P + P], zt[:, hg, i * P:i * P + P], ident[:])
                last.then_inc(c_zt, 1)

            def piece(k, b, what, e, m):
                g = FFN[k]
                n = g["n"]
                if what == "up":
                    u = NF * e + m
                    if u >= RING:
                        pe.wait_ge(f_g[k], NF * n * b + u - RING + 1)
                    pe.matmul(ps[:, 4 + u % RING, :], g["w1"][:, e, m * P:m * P + P], xt_tile(k, b)[:],
                              start=True, stop=True).then_inc(f_h[k], 1)
                if what == "down":
                    if m == 0:
                        pe.wait_ge(f_g[k], NF * n * b + NF * e + NF)
                        if e >= 1 and y_bank(k, b, e) == YBANK:
                            pe.wait_ge(f_acc[k], n * b + e)
                    for f in range(NF):
                        last = pe.matmul(ps[:, y_bank(k, b, e), m * P:m * P + P], hid[e % 2][:, f, m * P:m * P + P],
                                         g["w2"][:, e, f, :], start=(f == 0), stop=(f == NF - 1))
                    if m == NB - 1:
                        last.then_inc(f_y[k], 1)
                if what == "weights":
                    pe.wait_ge(f_comb[k], b + 1)
                    for t in range(NB):
                        last = pe.transpose(ps[0:n, SBANK, t * P:t * P + P], rt["comb"][:, t, 0:n], ident[:])
                    last.then_inc(f_ctps[k], 1)
                if what == "bias":
                    pe.wait_ge(f_ct[k], b + 1)
                    for t in range(NB):
                        last = pe.matmul(ps[:, SBANK, t * P:t * P + P], combt[0:n, t * P:t * P + P],
                                         g["b2"][0:n, :], start=True, stop=True)
                    last.then_inc(f_bias_ps[k], 1)

            def b_router(b):
                pe.wait_ge(xt_ready["b"], b + 1)
                for t in range(NB):
                    last = pe.matmul(ps[:, SBANK, t * E0:t * E0 + E0], xt_tile("b", b)[:, t * P:t * P + P], r0w[:],
                                     start=True, stop=True)
                last.then_inc(f_rps["b"], 1)

            def d_router(b):
                pe.wait_ge(xt_ready["d"], b + 1)
                for f in range(2):
                    pe.matmul(ps[:, RHBANK + f, :], r1w1[:, f * P:f * P + P], xtb[:], start=True,
                              stop=True).then_inc(d_rh_ps, 1)

            def d_logits(b, pieces):
                piece("d", b, *pieces[0])
                pe.wait_ge(d_rh, 2 * b + 2)
                for t in range(NB):
                    for f in range(2):
                        last = pe.matmul(ps[:, SBANK, t * E1:t * E1 + E1], rh[:, f, t * P:t * P + P],
                                         r1w2[:, f, :], start=(f == 0), stop=(f == 1))
                    if t == 1:
                        piece("d", b, *pieces[1])
                last.then_inc(f_rps["d"], 1)

            def phase_a(a, k, n):
                a_pair(a, 0)
                if k == "d":
                    pe.wait_ge(c_att, n + 1)
                a_pair(a, 1)
                a_pair(a, 2)
                pe.wait_ge(stats[k + "i"], 2 * n + 2)
                a_pair(a, 3, (k, n))
                pe.wait_ge(a_pair_act, 5 * a + 3)
                pieces = beside_attention(k, FFN[k]["n"])[0]
                if k == "d":
                    d_router(n)
                    d_logits(n, pieces)
                else:
                    b_router(n)
                    for what, e, m in pieces[:2]:
                        piece(k, n, what, e, m)
                for what, e, m in pieces[2:NF]:
                    piece(k, n, what, e, m)
                a_pair(a, NG)
                for what, e, m in pieces[NF:-NB]:
                    piece(k, n, what, e, m)
                a_scores(a, 0)
                for what, e, m in pieces[-NB:]:
                    piece(k, n, what, e, m)
                a_main(a, k, n)

            def experts_and_attention(k, b, c, done, following):
                for what, e, m in interleave(FFN[k]["n"])[done:]:
                    if what == "stack":
                        pe.wait_ge(c_v, c + 1)
                        pe.wait_ge(c_stack, 16 * 18 * c + 16 * 18)
                    elif what == "max":
                        c_max_scores(c, e)
                    elif what == "turn":
                        c_turn(c)
                    elif what != "split":
                        piece(k, b, what, e, m)
                c_main(c, k, b, following)

            def bridge(a, d):
                after = beside_attention("d", E1)[1] if d is not None else []
                for what, e, m in after[:NF - 1]:
                    piece("d", d, what, e, m)
                to_channels("c", a - 1)
                for what, e, m in after[NF - 1:]:
                    piece("d", d, what, e, m)
                pe.wait_ge(res_done["a"], a + 1)
                c_project(a - 1)
                c_project_keys(a - 1)
                to_channels("b", a)
                c_project_values(a - 1)
                if d is not None:
                    pe.wait_ge(f_acc["d"], E1 * d + E1)

            def phase_b(b, c, following):
                pe.wait_ge(xt_ready["b"], b + 1)
                for what, e, m in expert_pieces(E0 + 1)[:2]:
                    piece("b", b, what, e, m)
                b_router(b)
                experts_and_attention("b", b, c, 2, following)

            def phase_end(d, c):
                c_project(c)
                c_project_keys(c)
                c_project_values(c)
                to_channels("d", d)
                d_router(d)
                d_logits(d, expert_pieces(E1))
                experts_and_attention("d", d, c, 2, None)

            pe.wait_ge(s_ident, 16)
            to_channels("a", 0)
            pe.wait_ge(s_w, 16 * len(FIRST))
            for p in range(1 + NG):
                a_pair(0, p)
            a_scores(0, 0)
            a_main(0)
            to_channels("a", 1)
            phase_a(1, "b", 0)
            bridge(1, None)
            with pe.Fori(1, NSEQ - 1) as i:
                phase_b(i, i - 1, ("a", i + 1))
                pe.wait_ge(xt_ready["a"], i + 2)
                c_out(i - 1)
                phase_a(i + 1, "d", i - 1)
                bridge(i + 1, i - 1)
            phase_b(NSEQ - 1, NSEQ - 2, ("c", NSEQ - 1))
            pe.wait_ge(xt_ready["c"], NSEQ)
            c_out(NSEQ - 2)
            phase_end(NSEQ - 2, NSEQ - 1)
            c_out(NSEQ - 1)
            to_channels("d", NSEQ - 1)
            d_router(NSEQ - 1)
            d_logits(NSEQ - 1, expert_pieces(E1))
            for what, e, m in expert_pieces(E1)[2:]:
                piece("d", NSEQ - 1, what, e, m)

        @block.scalar
        def _(act):
            def copy_channels(k, b):
                act.wait_ge(xt_ps[k], b + 1)
                act.activation(xt_tile(k, b)[:], ps[:, xt_bank(k, b), :], ACT.Copy).then_inc(xt_ready[k], 1)

            def a_take(b, p):
                act.wait_ge(a_pair_ps, 5 * b + p + 1)
                if p >= 2:
                    act.wait_ge(a_ob, 5 * b + p - 1)
                    act.wait_ge(a_oa, 5 * b + p - 1)
                act.activation(rab[:, p % 2], ps[:, PAIRBANK[p]:PAIRBANK[p] + 2, :],
                               ACT.Copy).then_inc(a_pair_act, 1)
                if p < 2:
                    act.wait_ge(a_v_ps, 2 * b + p + 1)
                    act.activation(v0[:, 2 * p:2 * p + 2, :].rearrange("p t c -> p (t c)"), ps[:, 2, :],
                                   ACT.Copy).then_inc(a_v, 1)

            def a_high(b, p):
                act.wait_ge(a_oa, 5 * b + p + 1)
                act.wait_ge(a_ob, 5 * b + p + 1)
                if p >= 2:
                    act.wait_ge(a_scr, 160 * b + 32 * (p - 1))
                act.activation(hi[:, p % 2], oab[:, p % 2], ACT.Copy).then_inc(a_hi, 1)

            def a_main(b):
                def softmax(h):
                    for i in range(NB):
                        u = NB * h + i
                        n = P * (i + 1)
                        act.wait_ge(a_nm, UNITS * b + u + 1)
                        if i == 0 and h >= 2:
                            act.wait_ge(a_tr, H0 * b + h - 1)
                        act.activation(pb[:, h % 2, SEG[i]:SEG[i] + n], ps[:, u % 4, 0:n], ACT.Exp,
                                       bias=nm[:, u % 8:u % 8 + 1],
                                       accum_out=sums[:, h % 2, i:i + 1]).then_inc(a_exp, 1)

                softmax(0)
                for s in range(1, H0 + 2):
                    h = s - 2
                    if 0 <= h < H0:
                        act.wait_ge(a_tr, H0 * b + h + 1)
                        if h >= 3:
                            act.wait_ge(a_y_ps, (H0 // 2) * b + (h - 3) // 2 + 1)
                        turned = ps[:, 4:7, :].rearrange("p a c -> p (a c)")
                        start = TSEG[2] * (h % 2)
                        if h % 2:
                            act.activation(ptt[:, h % 3, 0:start], turned[:, 0:start],
                                           ACT.Copy).then_inc(a_pt_first, 1)
                        act.activation(ptt[:, h % 3, start:HEADW], turned[:, start:HEADW],
                                       ACT.Copy).then_inc(a_pt, 1)
                    if s < H0:
                        softmax(s)

            def c_values(b):
                act.wait_ge(c_v_ps, b + 1)
                act.activation(vs[:, :, :, 0:D1].rearrange("p t h d -> p (t h) d"),
                               ps[:, VBANK, :].rearrange("p (t d) -> p t d", d=D1), ACT.Copy).then_inc(c_v, 1)

            def c_main(b):
                for w in range(32):
                    act.wait_ge(c_s2, 32 * b + w + 1)
                    if w >= 4:
                        act.wait_ge(c_pv, 16 * b + (w - 4) // 2 + 1)
                    bank = 2 * (w % 3)
                    act.activation(pt1[:, w % 4], ps[:, bank:bank + 2, :], ACT.Exp, scale=SC1).then_inc(c_exp, 1)

            def piece(k, b, what, e, m):
                g = FFN[k]
                n = g["n"]
                if what == "up":
                    u = NF * e + m
                    act.wait_ge(f_h[k], NF * n * b + u + 1)
                    if m == 0 and e >= 2:
                        act.wait_ge(f_y[k], n * b + e - 1)
                    act.activation(hid[e % 2][:, m, :], ps[:, 4 + u % RING, :],
                                   ACT.Gelu_apprx_tanh if k == "b" else ACT.Gelu,
                                   bias=g["b1"][:, e, m:m + 1]).then_inc(f_g[k], 1)
                if what == "weights":
                    act.wait_ge(f_ctps[k], b + 1)
                    act.activation(combt[0:n, :], ps[0:n, SBANK, :], ACT.Copy).then_inc(f_ct[k], 1)

            def d_router(b):
                for f in range(2):
                    act.wait_ge(d_rh_ps, 2 * b + f + 1)
                    act.activation(rh[:, f, :], ps[:, RHBANK + f, :], ACT.Gelu, bias=r1b1[:, f:f + 1]).then_inc(d_rh, 1)

            def rope(a):
                for p in range(1 + NG):
                    a_take(a, p)
                    if p >= 1:
                        a_high(a, p - 1)
                a_high(a, NG)

            def phase_a(a, k, n):
                a_take(a, 0)
                a_take(a, 1)
                a_high(a, 0)
                a_take(a, 2)
                copy_channels(k, n)
                if k == "d":
                    d_router(n)
                a_high(a, 1)
                a_take(a, 3)
                ups = [(e, m) for what, e, m in beside_attention(k, FFN[k]["n"])[0] if what == "up"]
                for e, m in ups[:NF]:
                    piece(k, n, "up", e, m)
                a_high(a, 2)
                a_take(a, 4)
                for e, m in ups[NF:2 * NF]:
                    piece(k, n, "up", e, m)
                piece(k, n, "weights", 0, 0)
                a_high(a, 3)
                for e, m in ups[2 * NF:2 * NF + 2]:
                    piece(k, n, "up", e, m)
                a_high(a, 4)
                for e, m in ups[2 * NF + 2:]:
                    piece(k, n, "up", e, m)
                a_main(a)

            def bridge(a, d):
                if d is not None:
                    act.activation(nm[:], nm[:], ACT.Gelu)
                    for what, e, m in beside_attention("d", E1)[1]:
                        if what == "up":
                            piece("d", d, what, e, m)
                copy_channels("c", a - 1)
                copy_channels("b", a)
                c_values(a - 1)

            def experts_and_attention(k, b, c):
                for what, e, m in interleave(FFN[k]["n"]):
                    if what == "turn":
                        act.wait_ge(c_mt_ps, c + 1)
                        act.activation(mt[:], ps[0:48, SBANK, 0:T // 2].bitcast(BF16), ACT.Copy).then_inc(c_mt, 1)
                    elif what in ("up", "weights"):
                        piece(k, b, what, e, m)
                c_main(c)

            copy_channels("a", 0)
            act.wait_ge(s_w, 16 * len(FIRST))
            act.activation(wqa[:], wqa[:], ACT.Copy, scale=float(D0) ** -0.5).then_inc(s_wscaled, 1)
            act.activation(wqb[:], wqb[:], ACT.Copy, scale=float(D0) ** -0.5).then_inc(s_wscaled, 1)
            rope(0)
            a_main(0)
            act.wait_ge(s_wf, 16 * len(LATER))
            copy_channels("a", 1)
            phase_a(1, "b", 0)
            bridge(1, None)
            with act.Fori(1, NSEQ - 1) as i:
                experts_and_attention("b", i, i - 1)
                copy_channels("a", i + 1)
                phase_a(i + 1, "d", i - 1)
                bridge(i + 1, i - 1)
            experts_and_attention("b", NSEQ - 1, NSEQ - 2)
            copy_channels("c", NSEQ - 1)
            c_values(NSEQ - 1)
            copy_channels("d", NSEQ - 2)
            d_router(NSEQ - 2)
            experts_and_attention("d", NSEQ - 2, NSEQ - 1)
            copy_channels("d", NSEQ - 1)
            d_router(NSEQ - 1)
            for what, e, m in expert_pieces(E1):
                piece("d", NSEQ - 1, what, e, m)

        @block.vector
        def _(dve):
            CH = {"a": 2 + 4, "b": 2 + 16 + 4, "c": 2 + 5, "z": 1 + 4, "d": 2 + 15 + 4}
            done = {}

            def link(k, b, ins):
                done[k] += 1
                ins.then_inc(chain[k], 1)
                dve.wait_ge(chain[k], CH[k] * b + done[k])

            def norm_stats(k, which, b, src):
                for half in HALVES:
                    for t in range(NB)[half]:
                        if which == "ao":
                            dve.wait_ge(a_o_ps, NB * b + t + 1)
                            dve.nop(nofuse=True)
                        last = dve.bn_stats(st[:, t, :], src(t))
                    link(k, b, last)
                    dve.nop(nofuse=True)
                    for t in range(NB)[half]:
                        last = dve.bn_aggr(mv[:, t, :], st[:, t, :])
                    last.then_inc(stats[which], 1)

            def norm_in_stats(k, b):
                done[k] = 0
                if k == "a":
                    dve.wait_ge(a_in, 16 * b + 16)
                else:
                    dve.wait_ge(res_done["abcd"["abcd".index(k) - 1]], b + 1)
                norm_stats(k, k + "i", b, lambda t: SRC[k][:, t, :])

            def norm_in_scale(k, b):
                if k == "b" and not (isinstance(b, int) and b == 0):
                    dve.wait_ge(xt_ps["c"], b)
                for h, half in enumerate(HALVES):
                    dve.wait_ge(rs_ready[k + "i"], 2 * b + h + 1)
                    for t in range(NB)[half]:
                        last = dve.tensor_scalar(xn[:, t, :], SRC[k][:, t, :], mv[:, t, 0:1], rstd[:, t:t + 1],
                                                 ALU.subtract, ALU.mult)
                    last.then_inc(xn_ready[k], 1)

            def norm_in(k, b):
                norm_in_stats(k, b)
                norm_in_scale(k, b)

            def norm_out_scale(k, b, src, into, old, new, own=None):
                own = own or k
                for h, half in enumerate(HALVES):
                    dve.wait_ge(rs_ready[k + "o"], 2 * b + h + 1)
                    for t in range(NB)[half]:
                        last = dve.tensor_scalar(into[:, t, :], src(t), mv[:, t, 0:1], rstd[:, t:t + 1],
                                                 ALU.subtract, ALU.mult)
                    link(own, b, last)
                    last = dve.tensor_tensor(new[:, half], old[:, half], into[:, half], ALU.add)
                last.then_inc(res_done[k], 1)
                assert done[own] == CH[own], (own, done[own])

            def a_rotate(b, p):
                dve.wait_ge(a_pair_act, 5 * b + p + 1)
                if p > 0:
                    dve.wait_ge(a_oa, 5 * b + p)
                dve.tensor_tensor(t12[:, 0, :], rab[:, p % 2, 0, :], cos[:], ALU.mult)
                dve.tensor_tensor(t12[:, 1, :], rab[:, p % 2, 1, :], sin[:], ALU.mult).then_inc(a_t12, 1)
                dve.wait_ge(a_t12, 5 * b + p + 1)
                if p >= 2:
                    dve.wait_ge(a_hi, 5 * b + p - 1)
                    dve.wait_ge(a_lo, 5 * b + p - 1)
                dve.tensor_tensor(oab[:, p % 2, 0, :], t12[:, 0, :], t12[:, 1, :], ALU.subtract).then_inc(a_oa, 1)

            def a_low(b, p):
                dve.wait_ge(a_hi, 5 * b + p + 1)
                if p >= 2:
                    dve.wait_ge(a_scr, 160 * b + 32 * (p - 1))
                dve.tensor_tensor(lo[:, p % 2], oab[:, p % 2], hi[:, p % 2].bitcast(F32),
                                  ALU.subtract).then_inc(a_lo, 1)

            def a_maxima(b, h, blocks):
                for u in [NB * h + i for i in blocks]:
                    dve.wait_ge(a_s, UNITS * b + u + 1)
                    dve.tensor_reduce(nm[:, u % 8:u % 8 + 1], ps[:, u % 4, 0:P * (u % NB + 1)], AX_X, ALU.max,
                                      negate=True).then_inc(a_nm, 1)

            def a_normalise(b, h):
                dve.wait_ge(a_exp, UNITS * b + NB * h + NB)
                dve.reciprocal(rsum[:, h % 2, :], sums[:, h % 2, :]).then_inc(a_rs, 1)
                dve.wait_ge(a_rs, H0 * b + h + 1)
                for i in range(NB):
                    seg = pb[:, h % 2, SEG[i]:SEG[i] + P * (i + 1)]
                    last = dve.tensor_scalar(seg, seg, rsum[:, h % 2, i:i + 1], None, ALU.mult)
                last.then_inc(a_pn, 1)

            def a_values(b, j):
                dve.wait_ge(a_y_ps, (H0 // 2) * b + j + 1)
                dve.tensor_copy(yt[:, j, :], ps[:, 7, :]).then_inc(a_yt, 1)

            def a_main(b, c):
                for s in range(1, H0 + 1):
                    if s < H0:
                        a_maxima(b, s, (0, 1))
                    if s >= 2:
                        a_normalise(b, s - 1)
                    if s < H0:
                        a_maxima(b, s, (2, 3))
                    if s >= 4 and s % 2 == 0:
                        a_values(b, (s - 4) // 2)
                    if c is not None and s == H0 - 3:
                        norm_in_stats("c", c)
                    if c is not None and s == H0 - 2:
                        norm_in_scale("c", c)
                a_values(b, H0 // 2 - 1)

            def a_out(b):
                norm_stats("a", "ao", b, lambda t: ps[:, t, 0:C])
                norm_out_scale("a", b, lambda t: ps[:, t, 0:C], tmp, x0, x1)

            def c_split_first(b):
                dve.wait_ge(c_qk_ps, b + 1)
                link("c", b, dve.tensor_copy(parts[:, 0], ps[:, QKBANK:QKBANK + 2, :]))

            def c_split(b):
                dve.tensor_tensor(res[:], ps[:, QKBANK:QKBANK + 2, :], parts[:, 0], ALU.subtract).then_inc(c_res, 1)
                dve.wait_ge(c_res, b + 1)
                link("c", b, dve.tensor_copy(parts[:, 1], res[:]))
                dve.tensor_tensor(parts[:, 2], res[:], parts[:, 1], ALU.subtract).then_inc(c_parts, 1)

            def c_max(b, u):
                i, h = u // H1, u % H1
                dve.wait_ge(c_s1, 64 * b + u + 1)
                dve.tensor_reduce(nm1[:, i, h:h + 1], ps[:, u % 3, :], AX_X, ALU.max, negate=True).then_inc(c_nm, 1)

            def c_max_split(b):
                dve.wait_ge(c_nm, 64 * b + 64)
                link("c", b, dve.tensor_copy(nmp[:, :, 0, :], nm1[:]))
                link("c", b, dve.tensor_tensor(nm1r[:], nm1[:], nmp[:, :, 0, :], ALU.subtract))
                link("c", b, dve.tensor_copy(nmp[:, :, 1, :], nm1r[:]))
                dve.tensor_tensor(nmp[:, :, 2, :], nm1r[:], nmp[:, :, 1, :], ALU.subtract).then_inc(c_nmp, 1)

            def c_main(b, k, n):
                for hg in range(4):
                    dve.wait_ge(c_pv, 16 * b + 4 * hg + 4)
                    dve.tensor_copy(zt[:, hg, :], ps[:, 6 + hg % 2, :]).then_inc(c_z, 1)
                    if k is not None and hg == 1:
                        norm_in_stats(k, n)
                    if k is not None and hg == 2:
                        norm_in_scale(k, n)

            def c_out(b):
                dve.wait_ge(c_zt, b + 1)
                z = ps[:, 4:8, :].rearrange("p b c -> p (b c)").rearrange("p (n d) -> p n d", d=32)
                done["z"] = 0
                link("z", b, dve.reciprocal(rc1[:], z[:, :, D1]))
                att = zt[:, 0, :].rearrange("p (t c) -> p t c", c=C)
                dve.tensor_tensor(zt[:, 0, :].rearrange("p (n d) -> p n d", d=D1), z[:, :, 0:D1],
                                  rc1[:].unsqueeze(2).broadcast_to([P, NB * H1, D1]), ALU.mult).then_inc(c_att, 1)
                dve.wait_ge(c_att, b + 1)
                norm_stats("z", "co", b, lambda t: att[:, t, :])
                dve.wait_ge(c_x3, b + 1)
                norm_out_scale("c", b, lambda t: att[:, t, :], att, x3, x3, "z")

            def wide(j, r):
                return rm[:, j, :].unsqueeze(2).broadcast_to([P, NB, r])

            def routing_select(k, b):
                g = FFN[k]
                r = g["routed"]
                lg, eq, oh1, msk = (rt[x][:, :, 0:r] for x in ("lg", "eq", "oh1", "msk"))
                rk = ranks[:, 0:r].unsqueeze(1).broadcast_to([P, NB, r])
                dve.wait_ge(f_rps[k], b + 1)
                link(k, b, dve.tensor_tensor(lg, ps[:, SBANK, 0:NB * r].rearrange("p (t e) -> p t e", e=r),
                                             g["rb"][:].unsqueeze(1).broadcast_to([P, NB, r]), ALU.add))
                link(k, b, dve.tensor_reduce(rm[:, 0, :], lg, AX_X, ALU.max))
                last = dve.tensor_tensor(lg, lg, wide(0, r), ALU.subtract)
                if k == "d":
                    last.then_inc(f_lm[k], 1)
                    dve.wait_ge(f_lm[k], b + 1)
                else:
                    link(k, b, last)
                link(k, b, dve.scalar_tensor_tensor(out=eq, in0=lg, scalar=0.0, in1=rk, op0=ALU.is_ge,
                                                    op1=ALU.mult))
                link(k, b, dve.tensor_reduce(rm[:, 1, :], eq, AX_X, ALU.max))
                link(k, b, dve.tensor_tensor(oh1, eq, wide(1, r), ALU.is_equal))
                link(k, b, dve.scalar_tensor_tensor(out=msk, in0=oh1, scalar=-BIG, in1=lg,
                                                    op0=ALU.mult, op1=ALU.add))
                last = dve.tensor_reduce(rm[:, 2, :], msk, AX_X, ALU.max)
                if k == "b":
                    last.then_inc(f_lm[k], 1)
                    dve.wait_ge(f_lm[k], b + 1)
                else:
                    link(k, b, last)
                link(k, b, dve.tensor_tensor(eq, msk, wide(2, r), ALU.is_ge))
                link(k, b, dve.tensor_tensor(eq, eq, rk, ALU.mult))
                link(k, b, dve.tensor_reduce(rm[:, 3, :], eq, AX_X, ALU.max))
                link(k, b, dve.tensor_tensor(msk, eq, wide(3, r), ALU.is_equal))

            def routing_weights(k, b):
                r = FFN[k]["routed"]
                oh1, msk, ex, comb = (rt[x][:, :, 0:r] for x in ("oh1", "msk", "ex", "comb"))
                if k == "b":
                    second = rt["ex"][:, 0, 0:NB]
                    dve.wait_ge(f_ex[k], b + 1)
                    link(k, b, dve.tensor_scalar(rm[:, 0, :], second, 1.0, None, ALU.add))
                    link(k, b, dve.reciprocal(rm[:, 1, :], rm[:, 0, :]))
                    link(k, b, dve.tensor_tensor(rm[:, 3, :], second, rm[:, 1, :], ALU.mult))
                    link(k, b, dve.tensor_tensor(oh1, oh1, wide(1, r), ALU.mult))
                    link(k, b, dve.tensor_tensor(msk, msk, wide(3, r), ALU.mult))
                    dve.tensor_tensor(comb, oh1, msk, ALU.add).then_inc(f_comb[k], 1)
                else:
                    link(k, b, dve.tensor_tensor(msk, msk, oh1, ALU.add))
                    dve.wait_ge(f_ex[k], b + 1)
                    link(k, b, dve.tensor_tensor(msk, msk, ex, ALU.mult))
                    link(k, b, dve.tensor_reduce(rm[:, 0, :], ex, AX_X, ALU.add))
                    link(k, b, dve.reciprocal(rm[:, 1, :], rm[:, 0, :]))
                    dve.tensor_tensor(comb, msk, wide(1, r), ALU.mult).then_inc(f_comb[k], 1)

            def routing(k, b):
                routing_select(k, b)
                routing_weights(k, b)

            def piece(k, b, what, e, m):
                n = FFN[k]["n"]
                if what == "bias":
                    dve.wait_ge(f_comb[k], b + 1)
                    dve.wait_ge(f_bias_ps[k], b + 1)
                    dve.tensor_copy(acc[:].rearrange("p t c -> p (t c)"), ps[:, SBANK, :]).then_inc(f_bias[k], 1)
                    dve.wait_ge(f_bias[k], b + 1)
                if what == "down" and m == NB - 1:
                    dve.wait_ge(f_y[k], n * b + e + 1)
                    if e > 0:
                        dve.wait_ge(f_acc[k], n * b + e)
                    for t in range(NB):
                        last = dve.scalar_tensor_tensor(out=acc[:, t, :], in0=ps[:, y_bank(k, b, e), t * P:t * P + P],
                                                        scalar=rt["comb"][:, t, e:e + 1], in1=acc[:, t, :],
                                                        op0=ALU.mult, op1=ALU.add)
                    last.then_inc(f_acc[k], 1)

            def b_out(b):
                dve.wait_ge(f_acc["b"], (E0 + 1) * b + E0 + 1)
                norm_stats("b", "bo", b, lambda t: acc[:, t, :])
                if not (isinstance(b, int) and b == 0):
                    dve.wait_ge(c_x3, b)
                norm_out_scale("b", b, lambda t: acc[:, t, :], acc, x1, x2)

            def rope(a):
                for p in range(1 + NG):
                    a_rotate(a, p)
                    if p >= 1:
                        a_low(a, p - 1)
                a_low(a, NG)

            def phase_a(a, k, n, c):
                norm_in_stats(k, n)
                a_rotate(a, 0)
                if k == "b":
                    dve.wait_ge(xt_ps["a"], a + 1)
                norm_in_scale(k, n)
                a_rotate(a, 1)
                a_low(a, 0)
                a_rotate(a, 2)
                routing(k, n)
                a_low(a, 1)
                a_rotate(a, 3)
                a_low(a, 2)
                a_rotate(a, 4)
                a_low(a, 3)
                pieces = beside_attention(k, FFN[k]["n"])[0]
                second = pieces.index(("down", 1, 0))
                for what, e, m in pieces[:second]:
                    piece(k, n, what, e, m)
                a_low(a, 4)
                for what, e, m in pieces[second:-NB]:
                    piece(k, n, what, e, m)
                a_maxima(a, 0, range(NB))
                a_normalise(a, 0)
                for what, e, m in pieces[-NB:]:
                    piece(k, n, what, e, m)
                if k == "b":
                    b_out(n)
                a_main(a, c)

            def experts_and_attention(k, b, c):
                for what, e, m in interleave(FFN[k]["n"]):
                    if what == "max":
                        c_max(c, e)
                    elif what == "split":
                        c_max_split(c)
                    elif what in ("bias", "down"):
                        piece(k, b, what, e, m)

            def d_out(b):
                dve.wait_ge(f_acc["d"], E1 * b + E1)
                norm_stats("d", "do", b, lambda t: acc[:, t, :])
                norm_out_scale("d", b, lambda t: acc[:, t, :], acc, x3, x3)

            def bridge(a, d):
                a_out(a)
                norm_in("b", a)
                if d is not None:
                    for what, e, m in beside_attention("d", E1)[1]:
                        piece("d", d, what, e, m)
                    dve.wait_ge(f_acc["d"], E1 * d + E1)
                    norm_stats("d", "do", d, lambda t: acc[:, t, :])
                c_split_first(a - 1)
                c_split(a - 1)
                routing_select("b", a)
                if d is not None:
                    norm_out_scale("d", d, lambda t: acc[:, t, :], acc, x3, x3)
                routing_weights("b", a)

            def phase_b(b, c, k, n):
                experts_and_attention("b", b, c)
                b_out(b)
                c_main(c, k, n)

            dve.memset(rt["comb"][:, :, E0:E0 + 1], 1.0).then_inc(s_comb1, 1)
            dve.wait_ge(s_comb1, 1)
            dve.wait_ge(s_const, 4 + E0)
            dve.wait_ge(pool_dma, 16)
            norm_in("a", 0)
            dve.wait_ge(s_w, 16 * len(FIRST))
            rope(0)
            a_maxima(0, 0, range(NB))
            a_normalise(0, 0)
            a_main(0, None)
            a_out(0)
            norm_in("a", 1)
            dve.wait_ge(s_wf, 16 * len(LATER))
            phase_a(1, "b", 0, 0)
            bridge(1, None)
            with dve.Fori(1, NSEQ - 1) as i:
                phase_b(i, i - 1, "a", i + 1)
                c_out(i - 1)
                phase_a(i + 1, "d", i - 1, i)
                bridge(i + 1, i - 1)
            phase_b(NSEQ - 1, NSEQ - 2, "c", NSEQ - 1)
            c_out(NSEQ - 2)
            norm_in_stats("d", NSEQ - 2)
            c_split_first(NSEQ - 1)
            norm_in_scale("d", NSEQ - 2)
            c_split(NSEQ - 1)
            routing("d", NSEQ - 2)
            experts_and_attention("d", NSEQ - 2, NSEQ - 1)
            d_out(NSEQ - 2)
            c_main(NSEQ - 1, None, None)
            c_out(NSEQ - 1)
            norm_in("d", NSEQ - 1)
            routing("d", NSEQ - 1)
            for what, e, m in expert_pieces(E1):
                piece("d", NSEQ - 1, what, e, m)
            d_out(NSEQ - 1)

def kernel(**inputs):
    import numpy as np
    import concourse.bacc as bacc
    from concourse.bass_utils import run_bass_kernel_spmd

    v = {k: np.asarray(a) for k, a in inputs.items()}

    def blocks(w):
        return w.reshape(-1, P, w.shape[-1]).transpose(1, 0, 2)

    wq = v["L0_attn_Wq"].reshape(C, NG, 4, HALF, 2)
    wk = v["L0_attn_Wk"].reshape(C, KV0, HALF, 2)
    w1 = np.concatenate([v["L0_ffn_spec_w1"], v["L0_ffn_shared_w1"][None]])
    b1 = np.concatenate([v["L0_ffn_spec_b1"], v["L0_ffn_shared_b1"][None]])
    w2 = np.concatenate([v["L0_ffn_spec_w2"], v["L0_ffn_shared_w2"][None]])
    b2 = np.concatenate([v["L0_ffn_spec_b2"], v["L0_ffn_shared_b2"][None]])
    f32 = np.float32
    inv_freq = f32(1.0) / f32(10000.0) ** (np.arange(0, D0, 2, dtype=f32) / f32(D0))
    angle = (np.arange(T, dtype=f32)[None, :] * inv_freq[:, None]).astype(f32)
    bf16 = mybir.dt.np(BF16)
    arrays = {
        "x": v["L0_attn_x"].reshape(NSEQ, NB, P, C).transpose(0, 2, 1, 3),
        "wqa": wq[..., 0].reshape(C, NG, P), "wqb": wq[..., 1].reshape(C, NG, P),
        "wka": wk[..., 0].reshape(C, P), "wkb": wk[..., 1].reshape(C, P),
        "wv0": v["L0_attn_Wv"], "wo": blocks(v["L0_attn_Wo"]),
        "cos": np.tile(np.cos(angle), (4, 1)), "sin": np.tile(np.sin(angle), (4, 1)),
        "ident": np.eye(P, dtype=f32), "identb": np.eye(P, dtype=f32).astype(bf16),
        "maskb": np.triu(np.full((P, P), -BIG, f32), 1).astype(bf16),
        "f0w1": w1.transpose(2, 0, 1), "f0b1": b1.reshape(E0 + 1, NF, P).transpose(2, 0, 1),
        "f0w2": w2.transpose(2, 0, 1).reshape(NF, P, E0 + 1, C).transpose(1, 2, 0, 3), "f0b2": b2,
        "r0w": v["L0_ffn_router_w"].T, "r0b": np.broadcast_to(v["L0_ffn_router_b"], (P, E0)),
        "w1q": v["L1_attn_w_Q"], "w1k": v["L1_attn_w_K"], "w1v": v["L1_attn_w_V"],
        "f1w1": v["L1_ffn_We1"].transpose(1, 0, 2), "f1b1": v["L1_ffn_be1"].reshape(E1, NF, P).transpose(2, 0, 1),
        "f1w2": v["L1_ffn_We2"].reshape(E1, NF, P, C).transpose(2, 0, 1, 3), "f1b2": v["L1_ffn_be2"],
        "r1w1": v["L1_ffn_rW1"], "r1b1": v["L1_ffn_rb1"].reshape(2, P).T,
        "r1w2": blocks(v["L1_ffn_rW2"]), "r1b2": np.broadcast_to(v["L1_ffn_rb2"], (P, E1)),
    }
    nc = bacc.Bacc("TRN2", target_bir_lowering=False, num_devices=1)
    arrays = {k: np.ascontiguousarray(a) for k, a in arrays.items()}
    io = {k: nc.dram_tensor(k, a.shape, mybir.dt.from_np(a.dtype), kind="ExternalInput").ap()
          for k, a in arrays.items()}
    io["out"] = nc.dram_tensor("out", (NSEQ, P, NB, C), F32, kind="ExternalOutput").ap()
    sandwich_kernel(nc, io)
    r = run_bass_kernel_spmd(nc, [arrays], core_ids=[0])
    return r.results[0]["out"].transpose(0, 2, 1, 3).reshape(NSEQ, T, C)
```
